# Optimizing a Trainium2 kernel written in Bass

```python
import numpy as np
import jax
import jax.numpy as jnp

def _softmax(x, axis=-1):
    return jax.nn.softmax(x, axis=axis)

def _gelu(x):
    return jax.nn.gelu(x, approximate=True)

def _silu(x):
    return jax.nn.silu(x)

def _sigmoid(x):
    return jax.nn.sigmoid(x)

def _layernorm(x, axis=-1, eps=1e-05):
    m = jnp.mean(x, axis=axis, keepdims=True)
    v = jnp.var(x, axis=axis, keepdims=True)
    return (x - m) / jnp.sqrt(v + eps)

def _scatter_add(tgt, idx, src, axis=0):
    return tgt.at[idx].add(src)

def _segment_sum(src, seg, n):
    return jax.ops.segment_sum(src, seg, n)
kernel_name = 'mk_perceiver_d1_seqx_r4_03983b'

def setup_inputs(seed: int=0):
    np.random.seed(seed)
    _w = jnp.asarray

    def _rec_inputs():
        import jax
        import jax.numpy as jnp
        _rk = jax.random.key(seed)
        x = -0.0003929 + 0.9999 * jax.random.normal(jax.random.fold_in(_rk, 1), (16, 64, 256), jnp.float32)
        _lenS = 64 - jax.random.randint(jax.random.fold_in(_rk, 7), (16,), 0, max(1, 64 // 4) + 1, jnp.int32)
        _lenS2 = 1601 - jax.random.randint(jax.random.fold_in(_rk, 8), (16,), 0, max(1, 1601 // 4) + 1, jnp.int32)
        _ctx_1024P = jax.random.normal(jax.random.fold_in(_rk, 11), (16, 16, 256), jnp.float32)
        _ctx_1024c = jax.random.dirichlet(jax.random.fold_in(_rk, 511), 0.3 * jnp.ones((16,), jnp.float32), (16, 1601))
        _ctx_1024t = jnp.einsum('bsk,bkd->bsd', _ctx_1024c, _ctx_1024P)
        _ctx_1024t = _ctx_1024t * jax.lax.rsqrt(jnp.mean(jnp.square(_ctx_1024t)) + 1e-12) * 0.953939
        ctx_1024 = -0.000514642 + 1.00011 * (_ctx_1024t + 0.3 * jax.random.normal(jax.random.fold_in(_rk, 611), (16, 1601, 256), jnp.float32))
        return (x, ctx_1024)
    x, ctx_1024 = _rec_inputs()

    def _L0_xattn_setup():
        import jax, jax.numpy as jnp
        import numpy as np
        DIM = 256
        H = 16
        DH = 64
        INNER = H * DH
        SCALE = DH ** (-0.5)
        key = jax.random.key(seed)
        ks = jax.random.split(key, 6)
        B, L, R = (4, 1024, 128)
        x = jax.random.normal(ks[0], (B, L, DIM), dtype=jnp.float32)
        context = jax.random.normal(ks[1], (B, R, DIM), dtype=jnp.float32)
        s = DIM ** (-0.5)
        Wq = jax.random.normal(ks[2], (DIM, INNER), dtype=jnp.float32) * s
        Wk = jax.random.normal(ks[3], (DIM, INNER), dtype=jnp.float32) * s
        Wv = jax.random.normal(ks[4], (DIM, INNER), dtype=jnp.float32) * s
        Wo = jax.random.normal(ks[5], (INNER, DIM), dtype=jnp.float32) * INNER ** (-0.5)
        return {'x': x, 'context': context, 'Wq': Wq, 'Wk': Wk, 'Wv': Wv, 'Wo': Wo}
    _L0_xattn_all = _L0_xattn_setup()
    _L0_xattn_in = {k: v for k, v in _L0_xattn_all.items() if k in ('Wq', 'Wk', 'Wv', 'Wo')}
    del _L0_xattn_all

    def _L0_attn_setup():
        import jax, jax.numpy as jnp
        import numpy as np
        D_MODEL = 256
        N_HEADS = 16
        D_HEAD = D_MODEL // N_HEADS
        M_SLOPE = 0.5
        BATCH = 2
        SEQ = 512

        def _alibi_bias(n_heads, seq_len, m, dtype):
            slopes = m ** jnp.arange(n_heads, dtype=dtype)
            pos = jnp.arange(seq_len, dtype=dtype)
            dist = jnp.abs(pos[:, None] - pos[None, :])
            return -dist[None, :, :] * slopes[:, None, None]
        key = jax.random.key(seed)
        k1, k2, k3 = jax.random.split(key, 3)
        x = jax.random.normal(k1, (BATCH, SEQ, D_MODEL), dtype=jnp.float32)
        qkv_w = jax.random.normal(k2, (3 * D_MODEL, D_MODEL), dtype=jnp.float32) * (1.0 / np.sqrt(D_MODEL))
        qkv_b = jnp.zeros((3 * D_MODEL,), dtype=jnp.float32)
        out_w = jax.random.normal(k3, (D_MODEL, D_MODEL), dtype=jnp.float32) * (1.0 / np.sqrt(D_MODEL))
        out_b = jnp.zeros((D_MODEL,), dtype=jnp.float32)
        return {'x': x, 'qkv_w': qkv_w, 'qkv_b': qkv_b, 'out_w': out_w, 'out_b': out_b}
    _L0_attn_all = _L0_attn_setup()
    _L0_attn_in = {k: v for k, v in _L0_attn_all.items() if k in ('qkv_w', 'qkv_b', 'out_w', 'out_b')}
    del _L0_attn_all

    def _L0_ffn_setup():
        import jax, jax.numpy as jnp
        import numpy as np
        DIM = 256
        INTER = 256
        N_EXPERTS = 8
        TOPK = 2
        N_SHARED = 2
        key = jax.random.key(seed)
        ks = jax.random.split(key, 10)
        s = 0.02
        return {'x': jax.random.normal(ks[0], (4, 512, DIM), dtype=jnp.float32), 'gate_w': jax.random.normal(ks[1], (N_EXPERTS, DIM), dtype=jnp.float32) * s, 'gate_bias': jax.random.normal(ks[2], (N_EXPERTS,), dtype=jnp.float32) * s, 'w1': jax.random.normal(ks[3], (N_EXPERTS, INTER, DIM), dtype=jnp.float32) * s, 'w3': jax.random.normal(ks[4], (N_EXPERTS, INTER, DIM), dtype=jnp.float32) * s, 'w2': jax.random.normal(ks[5], (N_EXPERTS, DIM, INTER), dtype=jnp.float32) * s, 'sw1': jax.random.normal(ks[6], (N_SHARED * INTER, DIM), dtype=jnp.float32) * s, 'sw3': jax.random.normal(ks[7], (N_SHARED * INTER, DIM), dtype=jnp.float32) * s, 'sw2': jax.random.normal(ks[8], (DIM, N_SHARED * INTER), dtype=jnp.float32) * s}
    _L0_ffn_all = _L0_ffn_setup()
    _L0_ffn_in = {k: v for k, v in _L0_ffn_all.items() if k in ('gate_w', 'gate_bias', 'w1', 'w3', 'w2', 'sw1', 'sw3', 'sw2')}
    del _L0_ffn_all
    return {'x': x, 'ctx_1024': ctx_1024, 'L0_xattn_Wq': _L0_xattn_in['Wq'], 'L0_xattn_Wk': _L0_xattn_in['Wk'], 'L0_xattn_Wv': _L0_xattn_in['Wv'], 'L0_xattn_Wo': _L0_xattn_in['Wo'], 'L0_attn_qkv_w': _L0_attn_in['qkv_w'], 'L0_attn_qkv_b': _L0_attn_in['qkv_b'], 'L0_attn_out_w': _L0_attn_in['out_w'], 'L0_attn_out_b': _L0_attn_in['out_b'], 'L0_ffn_gate_w': _L0_ffn_in['gate_w'], 'L0_ffn_gate_bias': _L0_ffn_in['gate_bias'], 'L0_ffn_w1': _L0_ffn_in['w1'], 'L0_ffn_w3': _L0_ffn_in['w3'], 'L0_ffn_w2': _L0_ffn_in['w2'], 'L0_ffn_sw1': _L0_ffn_in['sw1'], 'L0_ffn_sw3': _L0_ffn_in['sw3'], 'L0_ffn_sw2': _L0_ffn_in['sw2']}

def reference(x, ctx_1024, L0_xattn_Wq, L0_xattn_Wk, L0_xattn_Wv, L0_xattn_Wo, L0_attn_qkv_w, L0_attn_qkv_b, L0_attn_out_w, L0_attn_out_b, L0_ffn_gate_w, L0_ffn_gate_bias, L0_ffn_w1, L0_ffn_w3, L0_ffn_w2, L0_ffn_sw1, L0_ffn_sw3, L0_ffn_sw2):
    import jax
    import jax.numpy as jnp

    def _L0_xattn_ref(x, context, Wq, Wk, Wv, Wo):
        import jax, jax.numpy as jnp
        import numpy as np
        DIM = 256
        H = 16
        DH = 64
        INNER = H * DH
        SCALE = DH ** (-0.5)
        B, L, _ = x.shape
        R = context.shape[1]
        q = (x @ Wq).reshape(B, L, H, DH).transpose(0, 2, 1, 3)
        k = (context @ Wk).reshape(B, R, H, DH).transpose(0, 2, 1, 3)
        v = (context @ Wv).reshape(B, R, H, DH).transpose(0, 2, 1, 3)
        scores = jnp.einsum('bhld,bhrd->bhlr', q, k) * SCALE
        attn = jax.nn.softmax(scores, axis=-1)
        out = jnp.einsum('bhlr,bhrd->bhld', attn, v)
        out = out.transpose(0, 2, 1, 3).reshape(B, L, INNER)
        return out @ Wo

    def _L0_attn_ref(x, qkv_w, qkv_b, out_w, out_b):
        import jax, jax.numpy as jnp
        import numpy as np
        D_MODEL = 256
        N_HEADS = 16
        D_HEAD = D_MODEL // N_HEADS
        M_SLOPE = 0.5
        BATCH = 2
        SEQ = 512

        def _alibi_bias(n_heads, seq_len, m, dtype):
            slopes = m ** jnp.arange(n_heads, dtype=dtype)
            pos = jnp.arange(seq_len, dtype=dtype)
            dist = jnp.abs(pos[:, None] - pos[None, :])
            return -dist[None, :, :] * slopes[:, None, None]
        batch, seq_len, d_model = x.shape
        qkv = x @ qkv_w.T + qkv_b
        qkv = qkv.reshape(batch, seq_len, N_HEADS, 3 * D_HEAD).transpose(0, 2, 1, 3)
        q, k, v = jnp.split(qkv, 3, axis=-1)
        scale = jnp.sqrt(jnp.asarray(D_HEAD, dtype=x.dtype))
        scores = jnp.einsum('bhid,bhjd->bhij', q, k) / scale
        scores = scores + _alibi_bias(N_HEADS, seq_len, M_SLOPE, x.dtype)[None]
        attn = jax.nn.softmax(scores, axis=-1)
        out = jnp.einsum('bhij,bhjd->bhid', attn, v)
        out = out.transpose(0, 2, 1, 3).reshape(batch, seq_len, d_model)
        return out @ out_w.T + out_b

    def _L0_ffn_ref(x, gate_w, gate_bias, w1, w3, w2, sw1, sw3, sw2):
        import jax, jax.numpy as jnp
        import numpy as np
        DIM = 256
        INTER = 256
        N_EXPERTS = 8
        TOPK = 2
        N_SHARED = 2
        shape = x.shape
        xt = x.reshape(-1, shape[-1])
        scores = jax.nn.softmax((xt @ gate_w.T).astype(jnp.float32), axis=-1)
        _, idx = jax.lax.top_k(scores + gate_bias, TOPK)
        weights = jnp.take_along_axis(scores, idx, axis=1).astype(x.dtype)
        y = jnp.zeros_like(xt)
        for e in range(N_EXPERTS):
            gate_e = jnp.sum(jnp.where(idx == e, weights, 0.0), axis=1)
            h = jax.nn.silu(xt @ w1[e].T) * (xt @ w3[e].T)
            y = y + gate_e[:, None] * (h @ w2[e].T)
        z = jax.nn.silu(xt @ sw1.T) * (xt @ sw3.T) @ sw2.T
        return (y + z).reshape(shape)
    x = x + _L0_xattn_ref(_layernorm(x, axis=-1), ctx_1024, L0_xattn_Wq, L0_xattn_Wk, L0_xattn_Wv, L0_xattn_Wo)
    x = x + _L0_attn_ref(_layernorm(x, axis=-1), L0_attn_qkv_w, L0_attn_qkv_b, L0_attn_out_w, L0_attn_out_b)
    x = x + _L0_ffn_ref(_layernorm(x, axis=-1), L0_ffn_gate_w, L0_ffn_gate_bias, L0_ffn_w1, L0_ffn_w3, L0_ffn_w2, L0_ffn_sw1, L0_ffn_sw3, L0_ffn_sw2)
    return x

_drawn_inputs = setup_inputs


def setup_inputs(seed=0):
    import zlib

    import numpy as np

    out = dict(_drawn_inputs(seed))
    spreads = {'L0_attn_qkv_b': (0.0, 0.1), 'L0_attn_out_b': (0.0, 0.1)}
    factors = {'L0_ffn_gate_w': 8.0,
     'L0_ffn_gate_bias': 8.0,
     'L0_ffn_w1': 8.0,
     'L0_ffn_w3': 8.0,
     'L0_ffn_w2': 8.0,
     'L0_ffn_sw1': 3.023,
     'L0_ffn_sw3': 3.012,
     'L0_ffn_sw2': 3.008}
    for name, (base, spread) in spreads.items():
        noise = np.random.default_rng([zlib.crc32(name.encode()), seed]).standard_normal(out[name].shape)
        drawn = base * np.exp(spread * noise) if base else spread * noise
        out[name] = jnp.asarray(drawn.astype(out[name].dtype))
    for name, factor in factors.items():
        out[name] = (out[name] * factor).astype(out[name].dtype)
    return out
```

```python
from contextlib import ExitStack

import numpy as np

import concourse.bass as bass
from concourse import mybir

ALU = mybir.AluOpType
ACT = mybir.ActivationFunctionType
AX = mybir.AxisListType
F32 = mybir.dt.float32
F32R = mybir.dt.float32r

P = 128
NB, T, D, S = 16, 64, 256, 1601
H, DH = 16, 64
KT = D // P
TOK = NB * T
NT = TOK // P
NG = 2
NR = 4
NQ = 4
QW = 400
SP = 1602
QE = [QW, QW, QW, SP - 3 * QW]
QV = [QW, QW, QW, S - 3 * QW]
NC = -(-S // P)
CW = [P] * (NC - 1) + [S - (NC - 1) * P]
CHUNKS = [range(0, 3), range(3, 6), range(6, 9), range(9, 13)]
ALL_GROUPS = NB * NG
SCALE = DH ** -0.5
EPS = 1e-5
H2, DH2 = 16, 16
SCALE2 = DH2 ** -0.5
NE, NSH, INTER = 8, 2, 256
NX = NE + NSH
BIG = 1e30


def cross_attention(nc, x, ctxT, ctx, Wq, WkT, Wv, Wo, ident_d, attn_outT):
    with ExitStack() as stack:
        def sb(name, shape, dt=F32):
            return stack.enter_context(nc.sbuf_tensor(name, shape, dt))

        def sem(name):
            return stack.enter_context(nc.semaphore(name))

        probs = sb("probs", [P, 2, NR, SP])
        pT_hi = sb("pT_hi", [P, 4, NR * P], F32R)
        pT_lo = sb("pT_lo", [P, 4, NR * P], F32R)
        ctx_raw = sb("ctx_raw", [P, NC, D])
        ctx_hi = sb("ctx_hi", [P, NC, D], F32R)
        ctx_lo = sb("ctx_lo", [P, NC, D], F32R)
        ctxT_raw = sb("ctxT_raw", [P, KT, SP])
        ctxT_hi = sb("ctxT_hi", [P, KT, SP], F32R)
        ctxT_lo = sb("ctxT_lo", [P, KT, SP], F32R)
        xT = sb("xT", [P, KT, TOK])
        wq = sb("wq", [P, KT, H * DH])
        wkT = sb("wkT", [P, H // 2, D])
        wv = sb("wv", [P, KT, H * DH])
        wo = sb("wo", [P, H // 2, D])
        ident = sb("ident", [P, P])
        qT = sb("qT", [P, 2, T])
        qk_hi = sb("qk_hi", [P, 2, KT, P], F32R)
        qk_lo = sb("qk_lo", [P, 2, KT, P], F32R)
        pcT = sb("pcT", [P, KT, NR * P])
        attT = sb("attT", [P, H // 2, T])
        ones = sb("ones", [P, D])
        bmax = sb("bmax", [P, 2, NQ])
        nmax = sb("nmax", [P, 2])
        psums = sb("psums", [P, 2, NQ])
        rsum = sb("rsum", [P, 2])
        rinv = sb("rinv", [P, 2])
        stats = sb("stats", [P, NT, 6])
        mv = sb("mv", [P, NT, 2])
        lnt = sb("lnt", [P, 6, NT])
        x_rows = probs[:, 1, 0:2, :].rearrange("p a b -> p (a b)")[:, 0:NT * D].rearrange(
            "p (n d) -> p n d", n=NT)

        ps_s = stack.enter_context(nc.psum_tensor("ps_s", [P, NQ, 512], F32))
        ps_t = stack.enter_context(nc.psum_tensor("ps_t", [P, 2, 512], F32))
        ps_o = stack.enter_context(nc.psum_tensor("ps_o", [P, KT, 512], F32))

        x_in = sem("x_in")
        w_in = sem("w_in")
        wvo_in = sem("wvo_in")
        ctxT_in = sem("ctxT_in")
        ctx_in = sem("ctx_in")
        ctx_tail_in = sem("ctx_tail_in")
        pad_set = sem("pad_set")
        ln_chain = sem("ln_chain")
        ln_var = sem("ln_var")
        ln_root = sem("ln_root")
        xn_ready = sem("xn_ready")
        xt_ps = sem("xt_ps")
        xT_ready = sem("xT_ready")
        ctxT_hi_ready = sem("ctxT_hi_ready")
        ctxT_ready = sem("ctxT_ready")
        ctx_hi_ready = sem("ctx_hi_ready")
        ctx_ready = sem("ctx_ready")
        scores_ready = sem("scores_ready")
        bmax_ready = sem("bmax_ready")
        nmax_ready = sem("nmax_ready")
        exp_done = sem("exp_done")
        rsum_ready = sem("rsum_ready")
        rinv_ready = sem("rinv_ready")
        probs_ready = sem("probs_ready")
        pT_ps = sem("pT_ps")
        pT_hi_ready = sem("pT_hi_ready")
        pT_ready = sem("pT_ready")
        pc_done = sem("pc_done")
        pcT_ready = sem("pcT_ready")
        q_ps = sem("q_ps")
        q_ready = sem("q_ready")
        qk_ps = sem("qk_ps")
        qk_hi_ready = sem("qk_hi_ready")
        qk_ready = sem("qk_ready")
        att_ps = sem("att_ps")
        att_ready = sem("att_ready")
        out_ps = sem("out_ps")
        out_ready = sem("out_ready")

        def wait(eng, s, count):
            if not isinstance(count, int) or count > 0:
                eng.wait_ge(s, count)

        def over_slots(eng, slot):
            for g0 in range(2):
                for r in range(NR):
                    slot(0, g0, r)
            with eng.Fori(0, ALL_GROUPS // 4 - 1) as i:
                for g0 in range(2, 6):
                    for r in range(NR):
                        slot(i, g0, r)
            for g0 in range(ALL_GROUPS - 2, ALL_GROUPS + 2):
                for r in range(NR):
                    slot(0, g0, r)

        def is_int(i):
            return isinstance(i, int)

        def has_scores(g0):
            return g0 < ALL_GROUPS

        def has_pc(g0):
            return 1 <= g0 <= ALL_GROUPS

        def has_att(g0):
            return g0 >= 2

        def has_next_q(g0, r):
            return 4 * g0 + r + 1 < 4 * ALL_GROUPS

        def keys(j):
            return slice(QW * j, QW * j + QE[j])

        ps_q = ps_s[:, 0, 0:T]
        ps_qk = ps_s[:, 0:2, T:T + KT * T].rearrange("p e (t q) -> p t e q", t=KT)
        ps_att = ps_s[:, 3, 0:4 * T]
        ps_out = ps_s[:, 3, 256:256 + KT * T]

        block = stack.enter_context(nc.Block())

        @block.sync
        def _(sp):
            xr = x.rearrange("(n p) d -> p n d", p=P)
            sp.dma_start(x_rows, xr).then_inc(x_in, 16)
            sp.dma_start(ident[:], ident_d).then_inc(x_in, 16)
            ctxT_v = ctxT.rearrange("b (t p) s -> b p t s", p=P)
            ctx_v = ctx[:, 0:(NC - 1) * P, :].rearrange("b (c p) d -> b p c d", p=P)
            sp.dma_start(ctxT_raw[:, :, 0:S], ctxT_v[0]).then_inc(ctxT_in, 16)
            sp.dma_start(wq[:], Wq.rearrange("(t p) n -> p t n", p=P)).then_inc(w_in, 16)
            sp.dma_start(wkT[:], WkT.rearrange("(t p) n -> p t n", p=P)).then_inc(w_in, 16)
            sp.dma_start(ctx_raw[:, 0:NC - 1, :], ctx_v[0]).then_inc(ctx_in, 16)
            sp.dma_start(ctx_raw[0:CW[-1], NC - 1, :], ctx[0, (NC - 1) * P:S, :]).then_inc(ctx_tail_in, 16)
            sp.dma_start(wv[:], Wv.rearrange("(t p) n -> p t n", p=P)).then_inc(wvo_in, 16)
            sp.dma_start(wo[:], Wo.rearrange("(t p) n -> p t n", p=P)).then_inc(wvo_in, 16)
            with sp.Fori(0, NB - 1) as b:
                sp.wait_ge(ctxT_ready, b * NQ + NQ)
                sp.dma_start(ctxT_raw[:, :, 0:S], ctxT_v[bass.ds(b + 1, 1)].rearrange("b p t s -> p (b t) s")
                             ).then_inc(ctxT_in, 16)
                sp.wait_ge(ctx_ready, b * NC + NC)
                sp.dma_start(ctx_raw[:, 0:NC - 1, :], ctx_v[bass.ds(b + 1, 1)].rearrange("b p c d -> p (b c) d")
                             ).then_inc(ctx_in, 16)
                sp.dma_start(ctx_raw[0:CW[-1], NC - 1, :],
                             ctx[bass.ds(b + 1, 1), (NC - 1) * P:S, :].rearrange("b p d -> (b p) d")
                             ).then_inc(ctx_tail_in, 16)

        @block.gpsimd
        def _(pool):
            pool.memset(ctxT_raw[:, :, S:SP], 0.0).then_inc(pad_set, 1)
            pool.memset(ones[:], 1.0).then_inc(pad_set, 1)
            pool.wait_ge(pad_set, 2)

            def split_ctxT(b):
                for j in range(NQ):
                    pool.wait_ge(ctxT_hi_ready, b * NQ + j + 1)
                    pool.tensor_tensor(ctxT_lo[:, :, keys(j)], ctxT_raw[:, :, keys(j)],
                                       ctxT_hi[:, :, keys(j)].bitcast(F32), ALU.subtract).then_inc(ctxT_ready, 1)

            def split_ctx(b):
                pool.wait_ge(ctx_in, b * 16 + 16)
                pool.wait_ge(ctx_tail_in, b * 16 + 16)
                for c in range(NC):
                    w = CW[c]
                    if not (is_int(b) and b == 0):
                        pool.wait_ge(pc_done, b * (NG * NC) + (c + 1 - NC))
                    pool.tensor_tensor(ctx_hi[0:w, c, :], ctx_raw[0:w, c, :], ones[0:w, :], ALU.mult
                                       ).then_inc(ctx_hi_ready, 1)
                    pool.wait_ge(ctx_hi_ready, b * NC + c + 1)
                    pool.tensor_tensor(ctx_lo[0:w, c, :], ctx_raw[0:w, c, :], ctx_hi[0:w, c, :].bitcast(F32),
                                       ALU.subtract).then_inc(ctx_ready, 1)

            split_ctxT(0)
            split_ctx(0)
            with pool.Fori(0, NB - 1) as b:
                split_ctxT(b + 1)
                split_ctx(b + 1)

        @block.scalar
        def _(act):
            act.wait_ge(ln_var, 1)
            act.activation(lnt[:, 1, :], lnt[:, 0, :], ACT.Sqrt).then_inc(ln_root, 1)

            def split_ctxT(b, j):
                act.wait_ge(ctxT_in, b * 16 + 16)
                act.activation(ctxT_hi[:, :, keys(j)], ctxT_raw[:, :, keys(j)], ACT.Copy
                               ).then_inc(ctxT_hi_ready, 1)

            act.wait_ge(pad_set, 1)
            for j in range(NQ):
                split_ctxT(0, j)

            def take_qk(n, n0):
                act.wait_ge(qk_ps, n + 1)
                act.activation(qk_hi[:, n0 % 2].rearrange("p t (e q) -> p t e q", e=2), ps_qk, ACT.Copy,
                               scale=SCALE).then_inc(qk_hi_ready, 1)

            take_qk(0, 0)

            def slot(i, g0, r):
                g, s = i * 4 + g0, i * 16 + (4 * g0 + r)
                chunk = i * (4 * NC) + NC * (g0 - 1)

                def take_pT(c):
                    w = CW[c]
                    act.wait_ge(pT_ps, chunk + c + 1)
                    wait(act, pc_done, chunk + c + 1 - 4)
                    act.activation(pT_hi[0:w, (NC * (g0 - 1) + c) % 4, :], ps_t[0:w, (NC * (g0 - 1) + c) % 2, :],
                                   ACT.Copy).then_inc(pT_hi_ready, 1)

                def exp(j):
                    if j == 0:
                        act.wait_ge(nmax_ready, s + 1)
                        wait(act, pT_ps, chunk)
                    act.activation(probs[:, g0 % 2, r, QW * j:QW * j + QV[j]], ps_s[:, j, 0:QV[j]], ACT.Exp,
                                   bias=nmax[:, s0 % 2:s0 % 2 + 1],
                                   accum_out=psums[:, s0 % 2, j:j + 1]).then_inc(exp_done, 1)

                s0 = 4 * g0 + r
                if has_pc(g0) and r == 0:
                    take_pT(0)
                    take_pT(1)
                if g0 % 2 == 1 and r == 3 and g0 < ALL_GROUPS - 1:
                    for j in range(NQ):
                        act.wait_ge(scores_ready, s * NQ + j + 1)
                        split_ctxT(i * 2 + (g0 // 2 + 1), j)
                for n, c in enumerate(CHUNKS[r]):
                    if has_pc(g0) and c + 2 < NC:
                        take_pT(c + 2)
                    if has_scores(g0):
                        exp(n)
                    if n == 1 and has_next_q(g0, r):
                        take_qk(s + 1, s0 + 1)
                if has_scores(g0) and len(CHUNKS[r]) < NQ:
                    exp(NQ - 1)

            over_slots(act, slot)

        @block.vector
        def _(dve):
            chain = [0]

            def link(ins):
                chain[0] += 1
                ins.then_inc(ln_chain, 1)
                dve.wait_ge(ln_chain, chain[0])

            dve.wait_ge(x_in, 32)
            for n in range(NT):
                last = dve.bn_stats(stats[:, n, :], x_rows[:, n, :])
            link(last)
            for n in range(NT):
                last = dve.bn_aggr(mv[:, n, :], stats[:, n, :])
            link(last)
            dve.tensor_scalar(lnt[:, 0, :], mv[:, :, 1], EPS, None, ALU.add).then_inc(ln_var, 1)
            dve.wait_ge(ln_var, 1)
            dve.wait_ge(ln_root, 1)
            link(dve.reciprocal(lnt[:, 2, :], lnt[:, 1, :]))
            link(dve.tensor_tensor(lnt[:, 3, :], lnt[:, 0, :], lnt[:, 2, :], ALU.mult))
            link(dve.tensor_tensor(lnt[:, 4, :], lnt[:, 3, :], lnt[:, 1, :], ALU.add))
            link(dve.tensor_scalar(lnt[:, 5, :], lnt[:, 4, :], 0.5, None, ALU.mult))
            link(dve.reciprocal(lnt[:, 2, :], lnt[:, 5, :]))
            for n in range(NT):
                dve.tensor_scalar(x_rows[:, n, :], x_rows[:, n, :], mv[:, n, 0:1], lnt[:, 2, n:n + 1],
                                  ALU.subtract, ALU.mult).then_inc(xn_ready, 1)
            for m in range(KT * NT // 4):
                dve.wait_ge(xt_ps, m + 1)
                dve.tensor_copy(xT[:, m // 2, 512 * (m % 2):512 * (m % 2) + 512], ps_s[:, m, :]
                                ).then_inc(xT_ready, 1)

            def take_q(n, n0):
                dve.wait_ge(q_ps, n + 1)
                dve.tensor_copy(qT[:, n0 % 2, :], ps_q).then_inc(q_ready, 1)

            def take_qk(n, n0):
                dve.wait_ge(qk_hi_ready, n + 1)
                for t in range(KT):
                    lo, hi = (a[:, n0 % 2, t].rearrange("p (e q) -> p e q", e=2) for a in (qk_lo, qk_hi))
                    last = dve.scalar_tensor_tensor(lo, ps_qk[:, t], SCALE, hi.bitcast(F32), ALU.mult,
                                                    ALU.subtract)
                last.then_inc(qk_ready, 1)

            take_q(0, 0)
            take_qk(0, 0)

            def slot(i, g0, r):
                s, s0 = i * 16 + (4 * g0 + r), 4 * g0 + r
                chunk = i * (4 * NC) + NC * (g0 - 1)

                def take_pT(c):
                    w, at = CW[c], NC * (g0 - 1) + c
                    dve.wait_ge(pT_hi_ready, chunk + c + 1)
                    dve.tensor_tensor(pT_lo[0:w, at % 4, :], ps_t[0:w, at % 2, :],
                                      pT_hi[0:w, at % 4, :].bitcast(F32), ALU.subtract).then_inc(pT_ready, 1)

                if has_att(g0) and r == 0:
                    dve.wait_ge(pc_done, chunk)
                    dve.tensor_copy(pcT[:], ps_o[:]).then_inc(pcT_ready, 1)
                if has_scores(g0):
                    for j in range(NQ):
                        dve.wait_ge(scores_ready, s * NQ + j + 1)
                        dve.tensor_reduce(bmax[:, s0 % 2, j:j + 1], ps_s[:, j, 0:QV[j]], AX.X, ALU.max
                                          ).then_inc(bmax_ready, 1)
                        if has_pc(g0) and r == 0 and j in (2, 3):
                            take_pT(j - 2)
                    dve.wait_ge(bmax_ready, s * NQ + NQ)
                    dve.tensor_reduce(nmax[:, s0 % 2:s0 % 2 + 1], bmax[:, s0 % 2, :], AX.X, ALU.max, negate=True
                                      ).then_inc(nmax_ready, 1)
                elif has_pc(g0) and r == 0:
                    take_pT(0)
                    take_pT(1)
                for n, c in enumerate(CHUNKS[r]):
                    if has_pc(g0) and c + 2 < NC:
                        take_pT(c + 2)
                    if n == 0 and has_next_q(g0, r):
                        take_q(s + 1, s0 + 1)
                    if n == 1 and has_next_q(g0, r):
                        take_qk(s + 1, s0 + 1)
                if has_att(g0) and r == 0:
                    dve.wait_ge(att_ps, i * 4 + (g0 - 1))
                    dve.tensor_copy(attT[:, 4 * (g0 % 2):4 * (g0 % 2) + 4, :],
                                    ps_att.rearrange("p (m q) -> p m q", m=4)).then_inc(att_ready, 1)
                if has_att(g0) and g0 % 2 == 1 and r == 1:
                    b = i * 2 + (g0 - 3) // 2
                    dve.wait_ge(out_ps, b + 1)
                    dve.tensor_copy(attn_outT[:, :, bass.ds(b * T, T)], ps_out.rearrange("p (t q) -> p t q", t=KT)
                                    ).then_inc(out_ready, 1)
                if has_scores(g0):
                    dve.wait_ge(exp_done, s * NQ + NQ)
                    dve.tensor_reduce(rsum[:, s0 % 2:s0 % 2 + 1], psums[:, s0 % 2, :], AX.X, ALU.add
                                      ).then_inc(rsum_ready, 1)
                    dve.wait_ge(rsum_ready, s + 1)
                    dve.reciprocal(rinv[:, s0 % 2:s0 % 2 + 1], rsum[:, s0 % 2:s0 % 2 + 1]).then_inc(rinv_ready, 1)
                    dve.wait_ge(rinv_ready, s + 1)
                    dve.tensor_scalar(probs[:, g0 % 2, r, 0:S], probs[:, g0 % 2, r, 0:S],
                                      rinv[:, s0 % 2:s0 % 2 + 1], None, ALU.mult).then_inc(probs_ready, 1)

            over_slots(dve, slot)

        @block.tensor
        def _(pe):
            for m in range(KT * NT // 4):
                for n in range(4):
                    tile = 4 * (m % 2) + n
                    pe.wait_ge(xn_ready, tile + 1)
                    last = pe.transpose(ps_s[:, m, P * n:P * n + P], x_rows[:, tile, P * (m // 2):P * (m // 2) + P],
                                        ident[:])
                last.then_inc(xt_ps, 1)

            def make_q(n, n0):
                pair = n0 % 8
                tok = bass.ds((n - pair) * (T // 8), T)
                for t in range(KT):
                    last = pe.matmul(ps_q, wq[:, t, P * pair:P * pair + P], xT[:, t, tok],
                                     start=t == 0, stop=t == KT - 1)
                last.then_inc(q_ps, 1)

            def make_qk(n, n0):
                pair = n0 % 8
                pe.wait_ge(q_ready, n + 1)
                for t in range(KT):
                    for e in range(2):
                        half = slice(DH * e, DH * e + DH)
                        last = pe.matmul(ps_qk[:, t, e, :], wkT[half, pair, P * t:P * t + P],
                                         qT[half, n0 % 2, :], start=True, stop=True)
                last.then_inc(qk_ps, 1)

            pe.wait_ge(xT_ready, KT * NT // 4)
            pe.wait_ge(w_in, 32)
            make_q(0, 0)
            make_qk(0, 0)

            def slot(i, g0, r):
                s, s0 = i * 16 + (4 * g0 + r), 4 * g0 + r
                chunk, chunk0 = i * (4 * NC) + NC * (g0 - 1), NC * (g0 - 1)

                def transpose_chunk(c):
                    w = CW[c]
                    if c == 0:
                        pe.wait_ge(probs_ready, i * 16 + 4 * g0)
                    wait(pe, pT_ready, chunk + c - 1)
                    for n in range(NR):
                        last = pe.transpose(ps_t[0:w, (chunk0 + c) % 2, P * n:P * n + P],
                                            probs[:, (g0 - 1) % 2, n, P * c:P * c + w], ident[:])
                    last.then_inc(pT_ps, 1)

                def multiply_chunk(c):
                    w, at = CW[c], (chunk0 + c) % 4
                    if c == 0:
                        wait(pe, pcT_ready, i * 4 + (g0 - 1))
                    if g0 % 2 == 1:
                        pe.wait_ge(ctx_ready, i * (2 * NC) + (g0 // 2 * NC + c + 1))
                    pe.wait_ge(pT_ready, chunk + c + 1)
                    for t in range(KT):
                        parts = [(ctx_hi, pT_hi), (ctx_lo, pT_hi), (ctx_hi, pT_lo)]
                        for n, (a, b) in enumerate(parts):
                            last = pe.matmul(ps_o[:, t, :], a[0:w, c, P * t:P * t + P], b[0:w, at, :],
                                             start=c == 0 and n == 0, stop=c == NC - 1 and n == 2)
                    last.then_inc(pc_done, 1)

                if has_scores(g0):
                    pe.wait_ge(qk_ready, s + 1)
                    for j in range(NQ):
                        if g0 % 2 == 0 and r == 0:
                            pe.wait_ge(ctxT_ready, i * 8 + (g0 // 2 * NQ + j + 1))
                        wait(pe, exp_done, s * NQ + (j + 1 - NQ))
                        if has_att(g0) and j == 3 and r == 1:
                            pe.wait_ge(att_ready, i * 4 + (g0 - 1))
                        if has_att(g0) and j == 3 and g0 % 2 == 1 and r == 2:
                            pe.wait_ge(out_ready, i * 2 + (g0 - 1) // 2)
                        parts = [(qk_hi, ctxT_hi), (qk_lo, ctxT_hi), (qk_hi, ctxT_lo)]
                        for t in range(KT):
                            for n, (a, b) in enumerate(parts):
                                last = pe.matmul(ps_s[:, j, 0:QE[j]], a[:, s0 % 2, t, :], b[:, t, keys(j)],
                                                 start=t == 0 and n == 0, stop=t == KT - 1 and n == 2)
                        last.then_inc(scores_ready, 1)
                        if has_pc(g0) and r == 0 and j in (1, 2):
                            transpose_chunk(j - 1)
                elif has_pc(g0) and r == 0:
                    transpose_chunk(0)
                    transpose_chunk(1)
                for n, c in enumerate(CHUNKS[r]):
                    if has_pc(g0):
                        if c + 2 < NC:
                            transpose_chunk(c + 2)
                        multiply_chunk(c)
                    if n == 0 and has_next_q(g0, r):
                        if has_scores(g0):
                            pe.wait_ge(exp_done, s * NQ + 1)
                        make_q(s + 1, s0 + 1)
                    if n == 1 and has_next_q(g0, r):
                        if has_scores(g0):
                            pe.wait_ge(exp_done, s * NQ + 2)
                        make_qk(s + 1, s0 + 1)
                    if n == 2 and has_att(g0) and r == 0:
                        if g0 == 2:
                            pe.wait_ge(wvo_in, 32)
                        pe.wait_ge(pcT_ready, i * 4 + (g0 - 1))
                        if has_scores(g0):
                            pe.wait_ge(exp_done, s * NQ + NQ)
                        for m in range(4):
                            pair = 4 * (g0 % 2) + m
                            for e in range(2):
                                for t in range(KT):
                                    col = DH * (2 * pair + e)
                                    row = T * (2 * m + e)
                                    last = pe.matmul(ps_att[DH * e:DH * e + DH, T * m:T * m + T],
                                                     wv[:, t, col:col + DH], pcT[:, t, row:row + T],
                                                     start=t == 0, stop=t == KT - 1)
                        last.then_inc(att_ps, 1)
                    if n == 2 and has_att(g0) and g0 % 2 == 1 and r == 1:
                        pe.wait_ge(att_ready, i * 4 + (g0 - 1))
                        if has_scores(g0):
                            pe.wait_ge(exp_done, s * NQ + NQ)
                        for t in range(KT):
                            for m in range(H // 2):
                                last = pe.matmul(ps_out[:, T * t:T * t + T], wo[:, m, P * t:P * t + P],
                                                 attT[:, m, :], start=m == 0, stop=m == H // 2 - 1)
                        last.then_inc(out_ps, 1)

            over_slots(pe, slot)


def self_attention_and_experts(nc, x, attn_outT, alibi_d, WA, bA, WB, bB, WV, bV, WoT, bo, gateT, gate_bias,
                               experts, ident_d, rank_d, out):
    with ExitStack() as stack:
        def sb(name, shape, dt=F32):
            return stack.enter_context(nc.sbuf_tensor(name, shape, dt))

        def sem(name):
            return stack.enter_context(nc.semaphore(name))

        x_in = sb("x_rows2", [P, NT, D])
        x1 = sb("x1", [P, NT, D])
        x2 = sb("x2", [P, NT, D])
        xn = sb("xn", [P, NT, D])
        xnT = sb("xnT", [P, KT, TOK])
        wa = sb("wa", [P, KT, 4 * P])
        wb = sb("wb", [P, KT, 4 * P])
        wvs = sb("wvs", [P, KT, 2 * P])
        woT = sb("woT", [P, KT, D])
        ba = sb("ba", [P, 4])
        bb = sb("bb", [P, 4])
        bv = sb("bv", [P, P])
        bout = sb("bout", [P, D])
        alibi = sb("alibi", [P, H2 * T])
        ident = sb("ident2", [P, P])
        rank = sb("rank", [P, NE])
        qa = sb("qa", [P, 4, TOK])
        kb = sb("kb", [P, 4, TOK])
        vs = sb("vs", [P, NB, P])
        pr = sb("pr", [P, 3, 4, 4, T])
        prT = sb("prT", [P, 2, 8, P])
        o_rows = sb("o_rows", [P, 2, D])
        oT = sb("oT", [P, 2, KT, P])
        pmax = sb("pmax", [P, 3, 16])
        psum_r = sb("psum_r", [P, 3, 16])
        pinv = sb("pinv", [P, 3, 16])
        stats = sb("stats2", [P, NT, 6])
        mv = sb("mv2", [P, NT, 2])
        lnt = sb("lnt2", [P, 6, NT])
        xnT_hi = sb("xnT_hi", [P, KT, TOK], F32R)
        xnT_lo = sb("xnT_lo", [P, KT, TOK], F32R)
        gw = sb("gw", [P, KT, NE])
        gb = sb("gb", [P, NE])
        gt = sb("gt", [P, 8, NT, NE])
        gr = sb("gr", [P, 6, NT])
        gates = sb("gates", [P, NT, NX])
        w_raw = sb("w_raw", [P, 2, 6, D])
        w_hi = sb("w_hi", [P, 2, 6, D], F32R)
        w_lo = sb("w_lo", [P, 2, 6, D], F32R)
        act_a = x_in[:, 0:4, :].rearrange("p (m a) d -> p m (a d)", m=2)
        hid = x_in[:, 4:8, :].rearrange("p (m a) d -> p m (a d)", m=2)
        hid_hi = sb("hid_hi", [P, 2, KT, 512], F32R)
        hid_lo = sb("hid_lo", [P, 2, KT, 512], F32R)

        ps_a = stack.enter_context(nc.psum_tensor("ps_a", [P, 4, 512], F32))
        ps_b = stack.enter_context(nc.psum_tensor("ps_b", [P, 2, 512], F32))
        ps_c = stack.enter_context(nc.psum_tensor("ps_c", [P, 2, 512], F32))

        x_ready = sem("x_ready2")
        wab_in = sem("wab_in")
        wv_in = sem("wv_in")
        wrest_in = sem("wrest_in")
        ew_in = [sem(f"ew_in{e}") for e in range(2)]
        chain_s = sem("dve_chain2")
        x1_ps = sem("x1_ps")
        x1_ready = sem("x1_ready")
        x1b_ready = sem("x1b_ready")
        var_ready = sem("var_ready2")
        root_ready = sem("root_ready2")
        xn_ready = sem("xn_ready2")
        xnT_ps = sem("xnT_ps")
        xnT_ready = sem("xnT_ready")
        ab_ps = sem("ab_ps")
        a_ready = sem("a_ready")
        b_ready = sem("b_ready")
        v_ps = sem("v_ps")
        v_ready = sem("v_ready")
        sc_ps = sem("sc_ps")
        sc_ready = sem("sc_ready")
        pmax_ready = sem("pmax_ready")
        shifted = sem("shifted")
        p_exp = sem("p_exp")
        psum_ready = sem("psum_ready")
        pinv_ready = sem("pinv_ready")
        p_ready = sem("p_ready")
        prT_ps = sem("prT_ps")
        prT_ready = sem("prT_ready")
        o_ps = sem("o_ps")
        o_ready = sem("o_ready")
        oT_ps = sem("oT_ps")
        oT_ready = sem("oT_ready")
        y_ps = sem("y_ps")
        x2_ready = sem("x2_ready")
        xnT_hi_ready = sem("xnT_hi_ready")
        xnT_lo_ready = sem("xnT_lo_ready")
        gl_ps = sem("gl_ps")
        gl_shifted = sem("gl_shifted")
        gl_exp = sem("gl_exp")
        gates_ready = sem("gates_ready")
        ewh_ready = sem("ewh_ready")
        ew_ready = sem("ew_ready")
        ab2_ps = sem("ab2_ps")
        silu_ready = sem("silu_ready")
        hid_ready = sem("hid_ready")
        hid_hi_ready = sem("hid_hi_ready")
        hid_lo_ready = sem("hid_lo_ready")
        ey_ps = sem("ey_ps")
        acc_ready = sem("acc_ready")
        stored = sem("stored")
        ones_set = sem("ones_set")

        def wait(eng, s, count):
            if not isinstance(count, int) or count > 0:
                eng.wait_ge(s, count)

        block = stack.enter_context(nc.Block())

        def probs_pairs(i):
            return [pr[:, i % 3, j, 2 * w:2 * w + 2, :].rearrange("p u k -> p (u k)")
                    for j in range(4) for w in range(2)]

        @block.sync
        def _(sp):
            sp.dma_start(ident[:], ident_d).then_inc(x_ready, 16)
            sp.dma_start(x_in[:], x.rearrange("(n p) d -> p n d", p=P)).then_inc(x_ready, 16)
            sp.dma_start(wa[:], WA.rearrange("(t p) n -> p t n", p=P)).then_inc(wab_in, 16)
            sp.dma_start(ba[:], bA).then_inc(wab_in, 16)
            sp.dma_start(wb[:], WB.rearrange("(t p) n -> p t n", p=P)).then_inc(wab_in, 16)
            sp.dma_start(bb[:], bB).then_inc(wab_in, 16)
            sp.dma_start(wvs[:], WV.rearrange("(t p) n -> p t n", p=P)).then_inc(wv_in, 16)
            for e in range(2):
                sp.dma_start(bv[T * e:T * e + T, :], bV[e].partition_broadcast(T)).then_inc(wv_in, 16)
            for e in range(2):
                sp.dma_start(alibi[T * e:T * e + T, :], alibi_d).then_inc(wv_in, 16)
            sp.dma_start(woT[:], WoT.rearrange("(t p) n -> p t n", p=P)).then_inc(wrest_in, 16)
            sp.dma_start(bout[:], bo.partition_broadcast(P)).then_inc(wrest_in, 16)
            sp.dma_start(gw[:], gateT.rearrange("(t p) n -> p t n", p=P)).then_inc(wrest_in, 16)
            sp.dma_start(gb[:], gate_bias.partition_broadcast(P)).then_inc(wrest_in, 16)
            sp.dma_start(rank[:], rank_d.partition_broadcast(P)).then_inc(wrest_in, 16)
            ew = experts.rearrange("x (w p) d -> x p w d", p=P)
            for e in range(2):
                sp.dma_start(w_raw[:, e], ew[e]).then_inc(ew_in[e], 16)
            with sp.Fori(0, NX // 2 - 1) as i:
                for e in range(2):
                    sp.wait_ge(ew_ready, i * 2 + (e + 1))
                    sp.dma_start(w_raw[:, e], ew[bass.ds(i * 2 + (2 + e), 1)].rearrange("x p w d -> p (x w) d")
                                 ).then_inc(ew_in[e], 16)
            outr = out.rearrange("(n p) d -> p n d", p=P)
            for h in range(2):
                for n in range(4):
                    sp.wait_ge(acc_ready, 8 * (NX - 1) + 4 * h + n + 1)
                    sp.dma_start(outr[:, 4 * h + n, :], x2[:, 4 * h + n, :]).then_inc(stored, 16)
            sp.wait_ge(stored, 16 * NT)

        @block.gpsimd
        def _(pool):
            pool.memset(gates[:, :, NE:NX], 1.0).then_inc(ones_set, 1)
            pool.wait_ge(wrest_in, 80)
            for n in range(NT):
                pool.wait_ge(x1_ready, n + 1)
                pool.tensor_tensor(x_in[:, n, :], x1[:, n, :], bout[:], ALU.add).then_inc(x1b_ready, 1)

            def normalise(i):
                pool.wait_ge(pinv_ready, i + 1)
                v = pr[:, i % 3].rearrange("p j u k -> p (j u) k")
                pool.tensor_tensor(v, v, pinv[:, i % 3, :].unsqueeze(2).to_broadcast([P, 16, T]), ALU.mult
                                   ).then_inc(p_ready, 1)

            for i in range(NT):
                pool.wait_ge(pmax_ready, i + 1)
                v = pr[:, i % 3].rearrange("p j u k -> p (j u) k")
                pool.tensor_tensor(v, v, pmax[:, i % 3, :].unsqueeze(2).to_broadcast([P, 16, T]), ALU.subtract
                                   ).then_inc(shifted, 1)
                if i >= 1:
                    normalise(i - 1)
            normalise(NT - 1)
            for m in range(4):
                t, cols = m // 2, slice(512 * (m % 2), 512 * (m % 2) + 512)
                pool.wait_ge(xnT_hi_ready, m + 1)
                pool.tensor_tensor(xnT_lo[:, t, cols], xnT[:, t, cols], xnT_hi[:, t, cols].bitcast(F32),
                                   ALU.subtract).then_inc(xnT_lo_ready, 1)

            def expert_weights(i, e):
                pool.wait_ge(ewh_ready, i * 2 + (e + 1))
                pool.tensor_tensor(w_lo[:, e % 2], w_raw[:, e % 2], w_hi[:, e % 2].bitcast(F32), ALU.subtract
                                   ).then_inc(ew_ready, 1)

            with pool.Fori(0, NX // 2) as i:
                for e in range(2):
                    expert_weights(i, e)

        @block.scalar
        def _(act):
            def roots(n):
                act.wait_ge(var_ready, n + 1)
                act.activation(lnt[:, 1, :], lnt[:, 0, :], ACT.Sqrt).then_inc(root_ready, 1)

            roots(0)
            act.wait_ge(wab_in, 64)
            for n in range(16):
                u, is_b, h = n // 4, n // 2 % 2, n % 2
                if not is_b:
                    act.wait_ge(ab_ps, n + 1)
                    act.activation(qa[:, u, 512 * h:512 * h + 512], ps_a[:, n % 4, :], ACT.Identity,
                                   bias=ba[:, u:u + 1]).then_inc(a_ready, 1)
            for i in range(NT + 1):
                if i < NT:
                    act.wait_ge(shifted, i + 1)
                    act.activation(pr[:, i % 3], pr[:, i % 3], ACT.Exp).then_inc(p_exp, 1)
                if i >= 1:
                    act.wait_ge(prT_ps, i)
                    act.activation(prT[:, (i - 1) % 2].rearrange("p (a b) q -> p a (b q)", a=2), ps_b[:], ACT.Copy
                                   ).then_inc(prT_ready, 1)
            roots(1)
            for m in range(4):
                t, cols = m // 2, slice(512 * (m % 2), 512 * (m % 2) + 512)
                act.wait_ge(xnT_ready, 4 + m + 1)
                act.activation(xnT_hi[:, t, cols], xnT[:, t, cols], ACT.Copy).then_inc(xnT_hi_ready, 1)
            act.wait_ge(gl_shifted, 1)
            act.activation(gt[:, 1], gt[:, 0], ACT.Exp).then_inc(gl_exp, 1)

            def split_weights(i, e):
                act.wait_ge(ew_in[e % 2], i * 16 + 16 * (e // 2 + 1))
                wait(act, ey_ps, i * 16 + 8 * (e - 1))
                act.activation(w_hi[:, e % 2], w_raw[:, e % 2], ACT.Copy).then_inc(ewh_ready, 1)

            def hidden(i, e, h):
                wait(act, ey_ps, i * 16 + (8 * (e - 1) + 4 * h + 4))
                for m in range(KT):
                    unit = i * 8 + (4 * e + 2 * h + m)
                    act.wait_ge(ab2_ps, unit + 1)
                    act.activation(act_a[:, m, :], ps_a[:, 2 * m, :], ACT.Silu).then_inc(silu_ready, 1)
                    act.wait_ge(hid_ready, unit + 1)
                    act.activation(hid_hi[:, h, m, :], hid[:, m, :], ACT.Copy).then_inc(hid_hi_ready, 1)

            def two_experts(i, last):
                for e in range(2):
                    hidden(i, e, 0)
                    if not (last and e == 1):
                        split_weights(i, e + 1)
                    hidden(i, e, 1)

            split_weights(0, 0)
            two_experts(0, False)
            with act.Fori(1, NX // 2 - 1) as i:
                two_experts(i, False)
            two_experts(NX // 2 - 1, True)

        @block.vector
        def _(dve):
            chain = [0]

            def link(ins):
                chain[0] += 1
                ins.then_inc(chain_s, 1)
                dve.wait_ge(chain_s, chain[0])

            def layernorm(rows, k):
                for n in range(NT):
                    last = dve.bn_stats(stats[:, n, :], rows[:, n, :])
                link(last)
                for n in range(NT):
                    last = dve.bn_aggr(mv[:, n, :], stats[:, n, :])
                link(last)
                dve.tensor_scalar(lnt[:, 0, :], mv[:, :, 1], EPS, None, ALU.add).then_inc(var_ready, 1)
                dve.wait_ge(var_ready, k + 1)
                dve.wait_ge(root_ready, k + 1)
                link(dve.reciprocal(lnt[:, 2, :], lnt[:, 1, :]))
                link(dve.tensor_tensor(lnt[:, 3, :], lnt[:, 0, :], lnt[:, 2, :], ALU.mult))
                link(dve.tensor_tensor(lnt[:, 4, :], lnt[:, 3, :], lnt[:, 1, :], ALU.add))
                link(dve.tensor_scalar(lnt[:, 5, :], lnt[:, 4, :], 0.5, None, ALU.mult))
                link(dve.reciprocal(lnt[:, 2, :], lnt[:, 5, :]))
                for n in range(NT):
                    dve.tensor_scalar(xn[:, n, :], rows[:, n, :], mv[:, n, 0:1], lnt[:, 2, n:n + 1],
                                      ALU.subtract, ALU.mult).then_inc(xn_ready, 1)

            def take_xnT(k):
                for m in range(4):
                    dve.wait_ge(xnT_ps, 4 * k + m + 1)
                    dve.tensor_copy(xnT[:, m // 2, 512 * (m % 2):512 * (m % 2) + 512], ps_a[:, m, :]
                                    ).then_inc(xnT_ready, 1)

            dve.wait_ge(x_ready, 32)
            for n in range(NT):
                dve.wait_ge(x1_ps, n + 1)
                dve.tensor_tensor(x1[:, n, :], ps_a[:, n % 4, 0:D], x_in[:, n, :], ALU.add).then_inc(x1_ready, 1)
            dve.wait_ge(x1_ready, NT)
            layernorm(x1, 0)
            take_xnT(0)
            dve.wait_ge(wab_in, 64)
            for n in range(16):
                u, is_b, h = n // 4, n // 2 % 2, n % 2
                if is_b:
                    dve.wait_ge(ab_ps, n + 1)
                    dve.tensor_scalar(kb[:, u, 512 * h:512 * h + 512], ps_a[:, n % 4, :], bb[:, u:u + 1], None,
                                      ALU.add).then_inc(b_ready, 1)
            dve.wait_ge(wv_in, 80)
            for n in range(NB // 4):
                dve.wait_ge(v_ps, n + 1)
                dve.tensor_tensor(vs[:, 4 * n:4 * n + 4, :], ps_b[:, n % 2, :].rearrange("p (b c) -> p b c", b=4),
                                  bv[:].unsqueeze(1).to_broadcast([P, 4, P]), ALU.add).then_inc(v_ready, 1)

            def scores(i):
                s = pr[:, i % 3]
                dve.wait_ge(sc_ps, i + 1)
                if i >= 3:
                    dve.wait_ge(prT_ps, i - 2)
                dve.scalar_tensor_tensor(s.rearrange("p j u k -> p j (u k)"), ps_a[:, :, 0:4 * T], SCALE2,
                                         alibi[:].rearrange("p (j c) -> p j c", j=4), ALU.mult, ALU.add
                                         ).then_inc(sc_ready, 1)
                dve.wait_ge(sc_ready, i + 1)
                dve.tensor_reduce(pmax[:, i % 3, :], s.rearrange("p j u k -> p (j u) k"), AX.X, ALU.max
                                  ).then_inc(pmax_ready, 1)

            def sums(i):
                dve.wait_ge(p_exp, i + 1)
                dve.tensor_reduce(psum_r[:, i % 3, :], pr[:, i % 3].rearrange("p j u k -> p (j u) k"), AX.X,
                                  ALU.add).then_inc(psum_ready, 1)
                dve.wait_ge(psum_ready, i + 1)
                dve.reciprocal(pinv[:, i % 3, :], psum_r[:, i % 3, :]).then_inc(pinv_ready, 1)

            def take_o(i):
                dve.wait_ge(o_ps, i + 1)
                dve.tensor_copy(o_rows[:, i % 2].rearrange("p (w o c) -> p o w c", w=2, o=2),
                                ps_c[:, :, 0:P].rearrange("p o (w c) -> p o w c", w=2)).then_inc(o_ready, 1)

            def take_oT(i):
                dve.wait_ge(oT_ps, i + 1)
                dve.tensor_copy(oT[:, i % 2], ps_c[:, 0, 0:KT * P].rearrange("p (t q) -> p t q", t=KT)
                                ).then_inc(oT_ready, 1)

            def residual(i):
                dve.wait_ge(x1b_ready, i + 1)
                dve.wait_ge(y_ps, i + 1)
                dve.tensor_tensor(x2[:, i, :], ps_c[:, 1, 0:D], x_in[:, i, :], ALU.add).then_inc(x2_ready, 1)

            scores(0)
            scores(1)
            for i in range(NT + 1):
                if i < NT:
                    sums(i)
                if i + 2 < NT:
                    scores(i + 2)
                if i >= 1:
                    take_oT(i - 1)
                    residual(i - 1)
                if i < NT:
                    take_o(i)
            dve.wait_ge(x2_ready, NT)
            layernorm(x2, 1)
            take_xnT(1)
            def over_e(a):
                return a.unsqueeze(2).to_broadcast([P, NT, NE])

            def over_n(a):
                return a.unsqueeze(1).to_broadcast([P, NT, NE])

            dve.wait_ge(gl_ps, 1)
            logits = ps_b[:, 0, 0:NT * NE].rearrange("p (n e) -> p n e", n=NT)
            link(dve.tensor_reduce(gr[:, 0, :], logits, AX.X, ALU.max))
            dve.tensor_tensor(gt[:, 0], logits, over_e(gr[:, 0, :]), ALU.subtract).then_inc(gl_shifted, 1)
            dve.wait_ge(gl_exp, 1)
            link(dve.tensor_reduce(gr[:, 1, :], gt[:, 1], AX.X, ALU.add))
            link(dve.reciprocal(gr[:, 2, :], gr[:, 1, :]))
            link(dve.tensor_tensor(gt[:, 2], gt[:, 1], over_e(gr[:, 2, :]), ALU.mult))
            dve.wait_ge(wrest_in, 80)
            link(dve.tensor_tensor(gt[:, 3], gt[:, 2], over_n(gb[:]), ALU.add))
            for k in range(2):
                biased, chosen = gt[:, 3], gt[:, 6 + k]
                link(dve.tensor_reduce(gr[:, 3, :], biased, AX.X, ALU.max))
                link(dve.tensor_tensor(gt[:, 4], biased, over_e(gr[:, 3, :]), ALU.is_ge))
                link(dve.tensor_tensor(gt[:, 5], gt[:, 4], over_n(rank[:]), ALU.mult))
                link(dve.tensor_reduce(gr[:, 4, :], gt[:, 5], AX.X, ALU.max))
                link(dve.tensor_tensor(chosen, gt[:, 5], over_e(gr[:, 4, :]), ALU.is_ge))
                if k == 0:
                    link(dve.scalar_tensor_tensor(biased, chosen, -BIG, biased, ALU.mult, ALU.add))
            link(dve.tensor_tensor(gt[:, 4], gt[:, 6], gt[:, 7], ALU.add))
            link(dve.tensor_tensor(gates[:, :, 0:NE], gt[:, 4], gt[:, 2], ALU.mult))

            def hidden(i, e, h):
                for m in range(KT):
                    unit = i * 8 + (4 * e + 2 * h + m)
                    dve.wait_ge(silu_ready, unit + 1)
                    dve.tensor_tensor(hid[:, m, :], act_a[:, m, :], ps_a[:, 2 * m + 1, :], ALU.mult
                                      ).then_inc(hid_ready, 1)
                    dve.wait_ge(hid_hi_ready, unit + 1)
                    dve.tensor_tensor(hid_lo[:, h, m, :], hid[:, m, :], hid_hi[:, h, m, :].bitcast(F32),
                                      ALU.subtract).then_inc(hid_lo_ready, 1)

            def accumulate(i, e, h):
                for n in range(4):
                    tile = 4 * h + n
                    dve.wait_ge(ey_ps, i * 16 + (8 * e + tile + 1))
                    wait(dve, acc_ready, i * 16 + (8 * e + tile + 1 - NT))
                    y = (ps_b, ps_c)[n // 2][:, n % 2, 0:D]
                    g = gates[:, tile, bass.ds(i * 2 + e, 1)]
                    dve.scalar_tensor_tensor(x2[:, tile, :], y, g, x2[:, tile, :], ALU.mult, ALU.add
                                             ).then_inc(acc_ready, 1)

            dve.wait_ge(ones_set, 1)
            hidden(0, 0, 0)
            hidden(0, 0, 1)
            accumulate(0, 0, 0)
            hidden(0, 1, 0)
            accumulate(0, 0, 1)
            hidden(0, 1, 1)
            accumulate(0, 1, 0)
            with dve.Fori(1, NX // 2) as i:
                hidden(i, 0, 0)
                accumulate(i - 1, 1, 1)
                hidden(i, 0, 1)
                accumulate(i, 0, 0)
                hidden(i, 1, 0)
                accumulate(i, 0, 1)
                hidden(i, 1, 1)
                accumulate(i, 1, 0)
            accumulate(NX // 2 - 1, 1, 1)

        @block.tensor
        def _(pe):
            pe.wait_ge(x_ready, 32)
            for n in range(NT):
                if n >= 4:
                    pe.wait_ge(x1_ready, n - 3)
                for t in range(KT):
                    last = pe.transpose(ps_a[:, n % 4, P * t:P * t + P], attn_outT[:, t, P * n:P * n + P], ident[:])
                last.then_inc(x1_ps, 1)

            def transpose_xn(k, free):
                for m in range(4):
                    for n in range(4):
                        tile = 4 * (m % 2) + n
                        pe.wait_ge(xn_ready, NT * k + tile + 1)
                        if n == 0:
                            free(m)
                        last = pe.transpose(ps_a[:, m, P * n:P * n + P], xn[:, tile, P * (m // 2):P * (m // 2) + P],
                                            ident[:])
                    last.then_inc(xnT_ps, 1)

            transpose_xn(0, lambda m: pe.wait_ge(x1_ready, NT))
            pe.wait_ge(wab_in, 64)
            for n in range(16):
                u, is_b, h = n // 4, n // 2 % 2, n % 2
                if n < 4:
                    pe.wait_ge(xnT_ready, 4)
                else:
                    pe.wait_ge(b_ready if is_b else a_ready, (n - 4) // 4 * 2 + h + 1)
                w = wb if is_b else wa
                for t in range(KT):
                    last = pe.matmul(ps_a[:, n % 4, :], w[:, t, P * u:P * u + P], xnT[:, t, 512 * h:512 * h + 512],
                                     start=t == 0, stop=t == KT - 1)
                last.then_inc(ab_ps, 1)
            pe.wait_ge(wv_in, 80)
            for b in range(NB):
                if b % 4 == 0 and b >= 8:
                    pe.wait_ge(v_ready, b // 4 - 1)
                for o in range(2):
                    for t in range(KT):
                        last = pe.matmul(ps_b[T * o:T * o + T, b // 4 % 2, P * (b % 4):P * (b % 4) + P],
                                         xnT[:, t, T * b:T * b + T], wvs[:, t, P * o:P * o + P],
                                         start=t == 0, stop=t == KT - 1)
                if b % 4 == 3:
                    last.then_inc(v_ps, 1)

            def scores(i):
                if i == 0:
                    pe.wait_ge(a_ready, 8)
                    pe.wait_ge(b_ready, 8)
                else:
                    pe.wait_ge(sc_ready, i)
                for u in range(4):
                    for e in range(2):
                        tok = slice(T * (2 * i + e), T * (2 * i + e) + T)
                        for j in range(4):
                            rows = slice(32 * j, 32 * j + DH2)
                            last = pe.matmul(ps_a[T * e:T * e + T, j, T * u:T * u + T], qa[rows, u, tok],
                                             kb[rows, u, tok], start=True, stop=True)
                last.then_inc(sc_ps, 1)

            def transpose_probs(i):
                pe.wait_ge(p_ready, i + 1)
                if i >= 1:
                    pe.wait_ge(prT_ready, i)
                else:
                    pe.wait_ge(v_ready, 4)
                for n, tile in enumerate(probs_pairs(i)):
                    last = pe.transpose(ps_b[:, n // 4, P * (n % 4):P * (n % 4) + P], tile, ident[:])
                last.then_inc(prT_ps, 1)

            def multiply_v(i):
                pe.wait_ge(prT_ready, i + 1)
                if i >= 1:
                    pe.wait_ge(x2_ready, i)
                for w in range(2):
                    for j in range(4):
                        for e in range(2):
                            for o in range(2):
                                half = slice(T * o, T * o + T)
                                col = DH2 * (4 * w + j)
                                last = pe.matmul(ps_c[T * e:T * e + T, o, col:col + DH2],
                                                 prT[half, i % 2, 2 * j + w, T * e:T * e + T],
                                                 vs[half, 2 * i + e, col:col + DH2], start=True, stop=True)
                last.then_inc(o_ps, 1)

            def transpose_o(i):
                pe.wait_ge(o_ready, i + 1)
                for t in range(KT):
                    last = pe.transpose(ps_c[:, 0, P * t:P * t + P], o_rows[:, i % 2, P * t:P * t + P], ident[:])
                last.then_inc(oT_ps, 1)

            def project(i):
                pe.wait_ge(oT_ready, i + 1)
                for t in range(KT):
                    last = pe.matmul(ps_c[:, 1, 0:D], oT[:, i % 2, t, :], woT[:, t, :], start=t == 0,
                                     stop=t == KT - 1)
                last.then_inc(y_ps, 1)

            pe.wait_ge(wrest_in, 80)
            scores(0)
            scores(1)
            for i in range(NT + 1):
                if i + 2 < NT:
                    scores(i + 2)
                if i >= 1:
                    transpose_o(i - 1)
                if i < NT:
                    transpose_probs(i)
                if i >= 1:
                    project(i - 1)
                if i < NT:
                    multiply_v(i)

            transpose_xn(1, lambda m: None)
            pe.wait_ge(xnT_ready, 8)
            for n in range(NT):
                for t in range(KT):
                    last = pe.matmul(ps_b[:, 0, NE * n:NE * n + NE], xnT[:, t, P * n:P * n + P], gw[:, t, :],
                                     start=t == 0, stop=t == KT - 1)
            last.then_inc(gl_ps, 1)

            def hidden(i, e, h):
                if h == 0:
                    pe.wait_ge(ew_ready, i * 2 + (e + 1))
                for m in range(KT):
                    unit = i * 8 + (4 * e + 2 * h + m)
                    wait(pe, hid_ready, unit - 1)
                    for k in range(2):
                        for t in range(KT):
                            parts = [(w_hi, xnT_hi), (w_lo, xnT_hi), (w_hi, xnT_lo)]
                            for n, (a, b) in enumerate(parts):
                                last = pe.matmul(ps_a[:, 2 * m + k, :], a[:, e, 2 * k + t, P * m:P * m + P],
                                                 b[:, t, 512 * h:512 * h + 512],
                                                 start=t == 0 and n == 0, stop=t == KT - 1 and n == 2)
                    last.then_inc(ab2_ps, 1)

            def outputs(i, e, h):
                unit = i * 8 + (4 * e + 2 * h)
                pe.wait_ge(hid_lo_ready, unit + 2)
                for n in range(4):
                    tile = 4 * h + n
                    wait(pe, acc_ready, i * 16 + (8 * e + tile + 1 - 4))
                    for t in range(KT):
                        parts = [(hid_hi, w_hi), (hid_lo, w_hi), (hid_hi, w_lo)]
                        for k, (a, b) in enumerate(parts):
                            last = pe.matmul((ps_b, ps_c)[n // 2][:, n % 2, 0:D], a[:, h, t, P * n:P * n + P],
                                             b[:, e, 4 + t, :], start=t == 0 and k == 0,
                                             stop=t == KT - 1 and k == 2)
                    last.then_inc(ey_ps, 1)

            pe.wait_ge(xnT_lo_ready, 4)
            pe.wait_ge(gl_shifted, 1)
            hidden(0, 0, 0)
            hidden(0, 0, 1)
            outputs(0, 0, 0)
            hidden(0, 1, 0)
            outputs(0, 0, 1)
            hidden(0, 1, 1)
            outputs(0, 1, 0)
            with pe.Fori(1, NX // 2) as i:
                hidden(i, 0, 0)
                outputs(i - 1, 1, 1)
                hidden(i, 0, 1)
                outputs(i, 0, 0)
                hidden(i, 1, 0)
                outputs(i, 0, 1)
                hidden(i, 1, 1)
                outputs(i, 1, 0)
            outputs(NX // 2 - 1, 1, 1)


def program(nc, x, ctxT, ctx, Wq, WkT, Wv, Wo, alibi, WA, bA, WB, bB, WV, bV, WoT, bo, gateT, gate_bias,
            experts, ident, rank, out):
    with nc.sbuf_tensor("attn_outT", [P, KT, TOK], F32) as attn_outT:
        cross_attention(nc, x, ctxT, ctx, Wq, WkT, Wv, Wo, ident, attn_outT)
        self_attention_and_experts(nc, x, attn_outT, alibi, WA, bA, WB, bB, WV, bV, WoT, bo, gateT, gate_bias,
                                   experts, ident, rank, out)


def layouts(v):
    qkv = v["L0_attn_qkv_w"].reshape(H2, 3 * DH2, D)
    qkv_b = v["L0_attn_qkv_b"].reshape(H2, 3 * DH2)

    def tiled(a):
        return a.reshape(4, P).T

    def even_odd(a):
        return a.reshape(2, 2, 4, *a.shape[1:]).transpose(1, 0, 2, *range(3, a.ndim + 2))

    pos = np.arange(T, dtype=np.float32)
    slopes = np.float32(0.5) ** np.arange(H2, dtype=np.float32)
    dist = -np.abs(pos[:, None] - pos[None, :])[:, None, :] * slopes[None, :, None]
    return {
        "x": v["x"].reshape(TOK, D),
        "ctxT": v["ctx_1024"].transpose(0, 2, 1),
        "ctx": v["ctx_1024"],
        "Wq": v["L0_xattn_Wq"],
        "WkT": v["L0_xattn_Wk"].T,
        "Wv": v["L0_xattn_Wv"],
        "Wo": v["L0_xattn_Wo"],
        "alibi": dist.reshape(T, 4, 4, T).transpose(0, 2, 1, 3).reshape(T, H2 * T),
        "WA": qkv[:, 0:2 * DH2].reshape(4 * P, D).T,
        "bA": tiled(qkv_b[:, 0:2 * DH2]),
        "WB": qkv[:, DH2:3 * DH2].reshape(4 * P, D).T,
        "bB": tiled(qkv_b[:, DH2:3 * DH2]),
        "WV": even_odd(qkv[:, 2 * DH2:]).reshape(D, D).T,
        "bV": even_odd(qkv_b[:, 2 * DH2:]).reshape(2, P),
        "WoT": v["L0_attn_out_w"].T,
        "bo": v["L0_attn_out_b"],
        "gateT": v["L0_ffn_gate_w"].T,
        "gate_bias": v["L0_ffn_gate_bias"],
        "experts": np.concatenate([
            np.concatenate([v["L0_ffn_w1"].transpose(0, 2, 1), v["L0_ffn_w3"].transpose(0, 2, 1),
                            v["L0_ffn_w2"].transpose(0, 2, 1)], axis=1),
            np.concatenate([v["L0_ffn_sw1"].reshape(NSH, INTER, D).transpose(0, 2, 1),
                            v["L0_ffn_sw3"].reshape(NSH, INTER, D).transpose(0, 2, 1),
                            v["L0_ffn_sw2"].T.reshape(NSH, INTER, D)], axis=1)], axis=0),
        "ident": np.eye(P, dtype=np.float32),
        "rank": np.arange(NE, 0, -1, dtype=np.float32),
    }


def kernel(**inputs):
    import numpy as _np
    import concourse.bacc as _bacc
    from concourse import mybir as _mybir
    from concourse.bass_utils import run_bass_kernel_spmd as _run

    nc = _bacc.Bacc("TRN2", target_bir_lowering=False, num_devices=1)
    arrays, args = {}, {}
    for name, a in layouts({k: _np.asarray(v) for k, v in inputs.items()}).items():
        a = _np.ascontiguousarray(a)
        arrays[f"in_{name}_dram"] = a
        args[name] = nc.dram_tensor(f"in_{name}_dram", a.shape, _mybir.dt.from_np(a.dtype), kind="ExternalInput").ap()
    out = nc.dram_tensor("out_0_dram", (TOK, D), _mybir.dt.float32, kind="ExternalOutput").ap()
    program(nc, out=out, **args)
    r = _run(nc, [arrays], core_ids=[0])
    return r.results[0]["out_0_dram"].reshape(NB, T, D)
```

```python
from contextlib import ExitStack

import numpy as np

import concourse.bass as bass
from concourse import mybir

ALU = mybir.AluOpType
ACT = mybir.ActivationFunctionType
AX = mybir.AxisListType
F32 = mybir.dt.float32
F32R = mybir.dt.float32r

P = 128
NB, T, D, S = 16, 64, 256, 1601
H, DH = 16, 64
KT = D // P
TOK = NB * T
NT = TOK // P
NG = 2
NR = 4
NQ = 4
QW = 400
SP = 1602
QE = [QW, QW, QW, SP - 3 * QW]
QV = [QW, QW, QW, S - 3 * QW]
NC = -(-S // P)
CW = [P] * (NC - 1) + [S - (NC - 1) * P]
CHUNKS = [range(0, 3), range(3, 6), range(6, 9), range(9, 13)]
ALL_GROUPS = NB * NG
SCALE = DH ** -0.5
EPS = 1e-5
H2, DH2 = 16, 16
SCALE2 = DH2 ** -0.5
NE, NSH, INTER = 8, 2, 256
NX = NE + NSH
BIG = 1e30


def cross_attention(nc, x, ctxT, ctx, Wq, WkT, Wv, Wo, ident_d, x1, x1_stats):
    with ExitStack() as stack:
        def sb(name, shape, dt=F32):
            return stack.enter_context(nc.sbuf_tensor(name, shape, dt))

        def sem(name):
            return stack.enter_context(nc.semaphore(name))

        probs = sb("probs", [P, 2, NR, SP])
        pT_hi = sb("pT_hi", [P, 4, NR * P], F32R)
        pT_lo = sb("pT_lo", [P, 4, NR * P], F32R)
        ctx_raw = sb("ctx_raw", [P, NC, D])
        ctx_hi = sb("ctx_hi", [P, NC, D], F32R)
        ctx_lo = sb("ctx_lo", [P, NC, D], F32R)
        ctxT_raw = sb("ctxT_raw", [P, KT, SP])
        ctxT_hi = sb("ctxT_hi", [P, KT, SP], F32R)
        ctxT_lo = sb("ctxT_lo", [P, KT, SP], F32R)
        xT = sb("xT", [P, KT, TOK])
        wq = sb("wq", [P, KT, H * DH])
        wkT = sb("wkT", [P, H // 2, D])
        wv = sb("wv", [P, KT, H * DH])
        wo = sb("wo", [P, H // 2, D])
        ident = sb("ident", [P, P])
        qT = sb("qT", [P, 2, T])
        qT_odd = sb("qT_odd", [P, H // 2, T])
        qk_hi = sb("qk_hi", [P, KT, P], F32R)
        qk_lo = sb("qk_lo", [P, KT, P], F32R)
        pcT = sb("pcT", [P, KT, NR * P])
        attT = sb("attT", [P, H // 2, 2, T])
        ones = sb("ones", [P, 1])
        bmax = sb("bmax", [P, 2, NQ])
        nmax = sb("nmax", [P, 2])
        psums = sb("psums", [P, 2, NQ])
        rsum = sb("rsum", [P, 2])
        rinv = sb("rinv", [P, 2])
        stats = sb("stats", [P, NT, 6])
        mv = sb("mv", [P, NT, 2])
        x_tile = sb("x_tile", [P, D])
        lnt = sb("lnt", [P, 6, NT])
        x_rows = probs[:, 1, 0:2, :].rearrange("p a b -> p (a b)")[:, 0:NT * D].rearrange(
            "p (n d) -> p n d", n=NT)

        ps_s = stack.enter_context(nc.psum_tensor("ps_s", [P, NQ, 512], F32))
        ps_t = stack.enter_context(nc.psum_tensor("ps_t", [P, 2, 512], F32))
        ps_o = stack.enter_context(nc.psum_tensor("ps_o", [P, KT, 512], F32))

        x_in = sem("x_in")
        w_in = sem("w_in")
        wvo_in = sem("wvo_in")
        ctxT_in = sem("ctxT_in")
        ctx_in = sem("ctx_in")
        ctx_tail_in = sem("ctx_tail_in")
        pad_set = sem("pad_set")
        ln_chain = sem("ln_chain")
        ln_var = sem("ln_var")
        ln_root = sem("ln_root")
        xn_ready = sem("xn_ready")
        xt_ps = sem("xt_ps")
        xT_ready = sem("xT_ready")
        ctxT_hi_ready = sem("ctxT_hi_ready")
        ctxT_ready = sem("ctxT_ready")
        ctx_hi_ready = sem("ctx_hi_ready")
        ctx_ready = sem("ctx_ready")
        scores_ready = sem("scores_ready")
        bmax_ready = sem("bmax_ready")
        nmax_ready = sem("nmax_ready")
        exp_done = sem("exp_done")
        rsum_ready = sem("rsum_ready")
        rinv_ready = sem("rinv_ready")
        probs_ready = sem("probs_ready")
        pT_ps = sem("pT_ps")
        pT_hi_ready = sem("pT_hi_ready")
        pT_ready = sem("pT_ready")
        pc_done = sem("pc_done")
        pcT_ready = sem("pcT_ready")
        q_ps = sem("q_ps")
        q_ready = sem("q_ready")
        qk_ps = sem("qk_ps")
        qk_hi_ready = sem("qk_hi_ready")
        qk_ready = sem("qk_ready")
        att_ps = sem("att_ps")
        att_ready = sem("att_ready")
        out_ps = sem("out_ps")
        out_ready = sem("out_ready")
        x_tile_in = sem("x_tile_in")
        x1_stats_ready = sem("x1_stats_ready")

        def wait(eng, s, count):
            if not isinstance(count, int) or count > 0:
                eng.wait_ge(s, count)

        def over_slots(eng, slot):
            for g0 in range(2):
                for r in range(NR):
                    slot(0, g0, r)
            with eng.Fori(0, ALL_GROUPS // 4 - 1) as i:
                for g0 in range(2, 6):
                    for r in range(NR):
                        slot(i, g0, r)
            for g0 in range(ALL_GROUPS - 2, ALL_GROUPS + 2):
                for r in range(NR):
                    slot(0, g0, r)

        def has_scores(g0):
            return g0 < ALL_GROUPS

        def has_pc(g0):
            return 1 <= g0 <= ALL_GROUPS

        def has_att(g0):
            return g0 >= 2

        def has_out(g0):
            return g0 >= 5 and g0 % 4 == 1

        def has_next_q(g0, r):
            return 4 * g0 + r + 1 < 4 * ALL_GROUPS

        def keys(j):
            return slice(QW * j, QW * j + QE[j])

        ps_q = ps_s[:, 0, 0:2 * T]
        ps_qk = ps_s[:, 1, 0:KT * P]
        ps_att = ps_s[:, 3, 0:4 * T]
        ps_out = ps_s[:, 3, 256:256 + D]

        def q_jobs(i, n0):
            return i * 8 + (n0 // 16 * 8 + min(n0 % 16, 7) + 1)

        x_tiles = x.rearrange("(n p) d -> p n d", p=P)
        block = stack.enter_context(nc.Block())

        @block.sync
        def _(sp):
            xr = x.rearrange("(n p) d -> p n d", p=P)
            sp.dma_start(x_rows, xr).then_inc(x_in, 16)
            sp.dma_start(ident[:], ident_d).then_inc(x_in, 16)
            ctxT_v = ctxT.rearrange("b (t p) s -> b p t s", p=P)
            ctx_v = ctx[:, 0:(NC - 1) * P, :].rearrange("b (c p) d -> b p c d", p=P)
            sp.dma_start(ctxT_raw[:, :, 0:S], ctxT_v[0]).then_inc(ctxT_in, 16)
            sp.dma_start(wq[:], Wq.rearrange("(t p) n -> p t n", p=P)).then_inc(w_in, 16)
            sp.dma_start(wkT[:], WkT.rearrange("(t p) n -> p t n", p=P)).then_inc(w_in, 16)
            sp.dma_start(ctx_raw[:, 0:NC - 1, :], ctx_v[0]).then_inc(ctx_in, 16)
            sp.dma_start(ctx_raw[0:CW[-1], NC - 1, :], ctx[0, (NC - 1) * P:S, :]).then_inc(ctx_tail_in, 16)
            sp.dma_start(wv[:], Wv.rearrange("(t p) n -> p t n", p=P)).then_inc(wvo_in, 16)
            sp.dma_start(wo[:], Wo.rearrange("(t p) n -> p t n", p=P)).then_inc(wvo_in, 16)
            with sp.Fori(0, NB - 1) as b:
                sp.wait_ge(ctxT_ready, b * NQ + NQ)
                sp.dma_start(ctxT_raw[:, :, 0:S], ctxT_v[bass.ds(b + 1, 1)].rearrange("b p t s -> p (b t) s")
                             ).then_inc(ctxT_in, 16)
                sp.wait_ge(ctx_ready, b * NC + NC)
                sp.dma_start(ctx_raw[:, 0:NC - 1, :], ctx_v[bass.ds(b + 1, 1)].rearrange("b p c d -> p (b c) d")
                             ).then_inc(ctx_in, 16)
                sp.dma_start(ctx_raw[0:CW[-1], NC - 1, :],
                             ctx[bass.ds(b + 1, 1), (NC - 1) * P:S, :].rearrange("b p d -> (b p) d")
                             ).then_inc(ctx_tail_in, 16)

        @block.gpsimd
        def _(pool):
            pool.memset(ctxT_raw[:, :, S:SP], 0.0).then_inc(pad_set, 1)
            pool.memset(ones[:], 1.0).then_inc(pad_set, 1)
            pool.wait_ge(pad_set, 2)

            def split_ctxT(b):
                for j in range(NQ):
                    pool.wait_ge(ctxT_hi_ready, b * NQ + j + 1)
                    pool.tensor_tensor(ctxT_lo[:, :, keys(j)], ctxT_raw[:, :, keys(j)],
                                       ctxT_hi[:, :, keys(j)].bitcast(F32), ALU.subtract).then_inc(ctxT_ready, 1)

            def split_ctx(b):
                pool.wait_ge(ctx_in, b * 16 + 16)
                pool.wait_ge(ctx_tail_in, b * 16 + 16)
                for c in range(NC):
                    w = CW[c]
                    if not (isinstance(b, int) and b == 0):
                        pool.wait_ge(pc_done, b * (NG * NC) + (c + 1 - NC))
                    pool.tensor_tensor(ctx_hi[0:w, c, :], ctx_raw[0:w, c, :], ones[0:w, :].to_broadcast([w, D]), ALU.mult
                                       ).then_inc(ctx_hi_ready, 1)
                    pool.wait_ge(ctx_hi_ready, b * NC + c + 1)
                    pool.tensor_tensor(ctx_lo[0:w, c, :], ctx_raw[0:w, c, :], ctx_hi[0:w, c, :].bitcast(F32),
                                       ALU.subtract).then_inc(ctx_ready, 1)

            split_ctxT(0)
            split_ctx(0)
            with pool.Fori(0, NB - 1) as b:
                split_ctxT(b + 1)
                split_ctx(b + 1)

        @block.scalar
        def _(act):
            act.wait_ge(ln_var, 1)
            act.activation(lnt[:, 1, :], lnt[:, 0, :], ACT.Sqrt).then_inc(ln_root, 1)

            def split_ctxT(b, j):
                act.wait_ge(ctxT_in, b * 16 + 16)
                act.activation(ctxT_hi[:, :, keys(j)], ctxT_raw[:, :, keys(j)], ACT.Copy
                               ).then_inc(ctxT_hi_ready, 1)

            act.wait_ge(pad_set, 1)
            for j in range(NQ):
                split_ctxT(0, j)

            def take_qk(n):
                act.wait_ge(qk_ps, n + 1)
                act.activation(qk_hi[:].rearrange("p t q -> p (t q)"), ps_qk, ACT.Copy, scale=SCALE
                               ).then_inc(qk_hi_ready, 1)

            take_qk(0)

            def slot(i, g0, r):
                g, s = i * 4 + g0, i * 16 + (4 * g0 + r)
                chunk = i * (4 * NC) + NC * (g0 - 1)

                def take_pT(c):
                    w = CW[c]
                    act.wait_ge(pT_ps, chunk + c + 1)
                    wait(act, pc_done, chunk + c + 1 - 4)
                    act.activation(pT_hi[0:w, (NC * (g0 - 1) + c) % 4, :], ps_t[0:w, (NC * (g0 - 1) + c) % 2, :],
                                   ACT.Copy).then_inc(pT_hi_ready, 1)

                def exp(j):
                    if j == 0:
                        act.wait_ge(nmax_ready, s + 1)
                        wait(act, pT_ps, chunk)
                    act.activation(probs[:, g0 % 2, r, QW * j:QW * j + QV[j]], ps_s[:, j, 0:QV[j]], ACT.Exp,
                                   bias=nmax[:, s0 % 2:s0 % 2 + 1],
                                   accum_out=psums[:, s0 % 2, j:j + 1]).then_inc(exp_done, 1)

                s0 = 4 * g0 + r
                if has_out(g0) and r == 0:
                    wait(act, out_ready, i + (g0 - 5) // 4)
                    act.dma_start(x_tile[:].unsqueeze(1), x_tiles[:, bass.ds(i + (g0 - 5) // 4, 1), :]
                                  ).then_inc(x_tile_in, 16)
                if has_pc(g0) and r == 0:
                    take_pT(0)
                    take_pT(1)
                if g0 % 2 == 1 and r == 3 and g0 < ALL_GROUPS - 1:
                    for j in range(NQ):
                        act.wait_ge(scores_ready, s * NQ + j + 1)
                        split_ctxT(i * 2 + (g0 // 2 + 1), j)
                for n, c in enumerate(CHUNKS[r]):
                    if has_scores(g0):
                        for j in ([0], [1, 2], [3], [])[n]:
                            exp(j)
                    if n == 1 and has_next_q(g0, r) and not has_pc(g0):
                        take_qk(s + 1)
                    if has_pc(g0) and c + 2 < NC:
                        take_pT(c + 2)
                    if n == 2 and has_next_q(g0, r) and has_pc(g0):
                        take_qk(s + 1)

            over_slots(act, slot)

        @block.vector
        def _(dve):
            chain = [0]

            def link(ins):
                chain[0] += 1
                ins.then_inc(ln_chain, 1)
                dve.wait_ge(ln_chain, chain[0])

            link(dve.memset(qT[:], 0.0))
            dve.wait_ge(x_in, 32)
            for n in range(NT):
                last = dve.bn_stats(stats[:, n, :], x_rows[:, n, :])
            link(last)
            for n in range(NT):
                last = dve.bn_aggr(mv[:, n, :], stats[:, n, :])
            link(last)
            dve.tensor_scalar(lnt[:, 0, :], mv[:, :, 1], EPS, None, ALU.add).then_inc(ln_var, 1)
            dve.wait_ge(ln_var, 1)
            dve.wait_ge(ln_root, 1)
            link(dve.reciprocal(lnt[:, 2, :], lnt[:, 1, :]))
            link(dve.tensor_tensor(lnt[:, 3, :], lnt[:, 0, :], lnt[:, 2, :], ALU.mult))
            link(dve.tensor_tensor(lnt[:, 4, :], lnt[:, 3, :], lnt[:, 1, :], ALU.add))
            link(dve.tensor_scalar(lnt[:, 5, :], lnt[:, 4, :], 0.5, None, ALU.mult))
            link(dve.reciprocal(lnt[:, 2, :], lnt[:, 5, :]))
            for n in range(NT):
                dve.tensor_scalar(x_rows[:, n, :], x_rows[:, n, :], mv[:, n, 0:1], lnt[:, 2, n:n + 1],
                                  ALU.subtract, ALU.mult).then_inc(xn_ready, 1)
            for m in range(KT * NT // 4):
                dve.wait_ge(xt_ps, m + 1)
                dve.tensor_copy(xT[:, m // 2, 512 * (m % 2):512 * (m % 2) + 512], ps_s[:, m, :]
                                ).then_inc(xT_ready, 1)

            def take_q(i, n, n0):
                if n0 // 8 % 2 == 0:
                    dve.wait_ge(q_ps, q_jobs(i, n0))
                    dve.tensor_copy(qT_odd[:, n0 % 8, :], ps_q[:, T:2 * T])
                    src = ps_q[:, 0:T]
                else:
                    dve.wait_ge(q_ready, n - 7)
                    dve.wait_ge(qk_ps, n)
                    src = qT_odd[:, n0 % 8, :]
                dve.tensor_copy(qT[0:DH, 0, :], src[0:DH])
                dve.tensor_copy(qT[DH:P, 1, :], src[DH:P]).then_inc(q_ready, 1)

            def take_qk(n):
                dve.wait_ge(qk_hi_ready, n + 1)
                lo, hi = (a[:].rearrange("p t q -> p (t q)") for a in (qk_lo, qk_hi))
                dve.scalar_tensor_tensor(lo, ps_qk, SCALE, hi.bitcast(F32), ALU.mult, ALU.subtract
                                         ).then_inc(qk_ready, 1)

            take_q(0, 0, 0)
            take_qk(0)

            def slot(i, g0, r):
                s, s0 = i * 16 + (4 * g0 + r), 4 * g0 + r
                chunk = i * (4 * NC) + NC * (g0 - 1)

                def take_pT(c):
                    w, at = CW[c], NC * (g0 - 1) + c
                    dve.wait_ge(pT_hi_ready, chunk + c + 1)
                    dve.tensor_tensor(pT_lo[0:w, at % 4, :], ps_t[0:w, at % 2, :],
                                      pT_hi[0:w, at % 4, :].bitcast(F32), ALU.subtract).then_inc(pT_ready, 1)

                if has_att(g0) and r == 0:
                    dve.wait_ge(pc_done, chunk)
                    dve.tensor_copy(pcT[:], ps_o[:]).then_inc(pcT_ready, 1)
                if has_scores(g0):
                    for j in range(NQ):
                        dve.wait_ge(scores_ready, s * NQ + j + 1)
                        dve.tensor_reduce(bmax[:, s0 % 2, j:j + 1], ps_s[:, j, 0:QV[j]], AX.X, ALU.max
                                          ).then_inc(bmax_ready, 1)
                        if has_pc(g0) and r == 0 and j == 2:
                            take_pT(0)
                    dve.wait_ge(bmax_ready, s * NQ + NQ)
                    dve.tensor_reduce(nmax[:, s0 % 2:s0 % 2 + 1], bmax[:, s0 % 2, :], AX.X, ALU.max, negate=True
                                      ).then_inc(nmax_ready, 1)
                    if has_pc(g0) and r == 0:
                        take_pT(1)
                elif has_pc(g0) and r == 0:
                    take_pT(0)
                    take_pT(1)
                for n, c in enumerate(CHUNKS[r]):
                    if has_pc(g0) and c + 2 < NC:
                        take_pT(c + 2)
                    if n == 0 and has_next_q(g0, r):
                        take_q(i, s + 1, s0 + 1)
                    if n == 2 and has_next_q(g0, r):
                        take_qk(s + 1)
                if has_att(g0) and r == 0:
                    dve.wait_ge(att_ps, i * 4 + (g0 - 1))
                    dve.tensor_copy(attT[:, 4 * (g0 % 2):4 * (g0 % 2) + 4, (g0 - 2) // 2 % 2, :],
                                    ps_att.rearrange("p (m q) -> p m q", m=4)).then_inc(att_ready, 1)
                if has_out(g0) and r == 1:
                    dve.wait_ge(out_ps, i + (g0 - 1) // 4)
                    dve.wait_ge(x_tile_in, i * 16 + 16 * ((g0 - 1) // 4))
                    tile = bass.ds(i + (g0 - 5) // 4, 1)
                    dve.tensor_tensor(x1[:, tile, :], ps_out.unsqueeze(1), x_tile[:].unsqueeze(1), ALU.add
                                      ).then_inc(out_ready, 1)
                    dve.wait_ge(out_ready, i + (g0 - 1) // 4)
                    dve.bn_stats(x1_stats[:, tile, :], x1[:, tile, :]).then_inc(x1_stats_ready, 1)
                if has_scores(g0):
                    dve.wait_ge(exp_done, s * NQ + NQ)
                    dve.tensor_reduce(rsum[:, s0 % 2:s0 % 2 + 1], psums[:, s0 % 2, :], AX.X, ALU.add
                                      ).then_inc(rsum_ready, 1)
                    dve.wait_ge(rsum_ready, s + 1)
                    dve.reciprocal(rinv[:, s0 % 2:s0 % 2 + 1], rsum[:, s0 % 2:s0 % 2 + 1]).then_inc(rinv_ready, 1)
                    dve.wait_ge(rinv_ready, s + 1)
                    dve.tensor_scalar(probs[:, g0 % 2, r, 0:S], probs[:, g0 % 2, r, 0:S],
                                      rinv[:, s0 % 2:s0 % 2 + 1], None, ALU.mult).then_inc(probs_ready, 1)

            over_slots(dve, slot)

        @block.tensor
        def _(pe):
            for m in range(KT * NT // 4):
                for n in range(4):
                    tile = 4 * (m % 2) + n
                    pe.wait_ge(xn_ready, tile + 1)
                    last = pe.transpose(ps_s[:, m, P * n:P * n + P], x_rows[:, tile, P * (m // 2):P * (m // 2) + P],
                                        ident[:])
                last.then_inc(xt_ps, 1)

            def make_q(n, n0):
                tok = bass.ds((n - n0 % 8) * (T // 8), 2 * T)
                for t in range(KT):
                    last = pe.matmul(ps_q, wq[:, t, P * (n0 % 8):P * (n0 % 8) + P], xT[:, t, tok],
                                     start=t == 0, stop=t == KT - 1)
                last.then_inc(q_ps, 1)

            def make_qk(n, n0):
                pe.wait_ge(q_ready, n + 1)
                for t in range(KT):
                    last = pe.matmul(ps_qk[:, P * t:P * t + P], wkT[:, n0 % 8, P * t:P * t + P],
                                     qT[:].rearrange("p e q -> p (e q)"), start=True, stop=True)
                last.then_inc(qk_ps, 1)

            pe.wait_ge(xT_ready, KT * NT // 4)
            pe.wait_ge(w_in, 32)
            make_q(0, 0)
            make_qk(0, 0)

            def slot(i, g0, r):
                s, s0 = i * 16 + (4 * g0 + r), 4 * g0 + r
                chunk, chunk0 = i * (4 * NC) + NC * (g0 - 1), NC * (g0 - 1)

                def transpose_chunk(c):
                    w = CW[c]
                    if c == 0:
                        pe.wait_ge(probs_ready, i * 16 + 4 * g0)
                    wait(pe, pT_ready, chunk + c - 1)
                    for n in range(NR):
                        last = pe.transpose(ps_t[0:w, (chunk0 + c) % 2, P * n:P * n + P],
                                            probs[:, (g0 - 1) % 2, n, P * c:P * c + w], ident[:])
                    last.then_inc(pT_ps, 1)

                def multiply_chunk(c):
                    w, at = CW[c], (chunk0 + c) % 4
                    if c == 0:
                        wait(pe, pcT_ready, i * 4 + (g0 - 1))
                    if g0 % 2 == 1:
                        pe.wait_ge(ctx_ready, i * (2 * NC) + (g0 // 2 * NC + c + 1))
                    pe.wait_ge(pT_ready, chunk + c + 1)
                    for t in range(KT):
                        parts = [(ctx_hi, pT_hi), (ctx_lo, pT_hi), (ctx_hi, pT_lo)]
                        for n, (a, b) in enumerate(parts):
                            last = pe.matmul(ps_o[:, t, :], a[0:w, c, P * t:P * t + P], b[0:w, at, :],
                                             start=c == 0 and n == 0, stop=c == NC - 1 and n == 2)
                    last.then_inc(pc_done, 1)

                if has_scores(g0):
                    pe.wait_ge(qk_ready, s + 1)
                    for j in range(NQ):
                        if g0 % 2 == 0 and r == 0:
                            pe.wait_ge(ctxT_ready, i * 8 + (g0 // 2 * NQ + j + 1))
                        wait(pe, exp_done, s * NQ + (j + 1 - NQ))
                        if has_att(g0) and j == 3 and r == 1:
                            pe.wait_ge(att_ready, i * 4 + (g0 - 1))
                        if has_out(g0) and j == 3 and r == 2:
                            pe.wait_ge(out_ready, i + (g0 - 1) // 4)
                        parts = [(qk_hi, ctxT_hi), (qk_lo, ctxT_hi), (qk_hi, ctxT_lo)]
                        for t in range(KT):
                            for n, (a, b) in enumerate(parts):
                                last = pe.matmul(ps_s[:, j, 0:QE[j]], a[:, t, :], b[:, t, keys(j)],
                                                 start=t == 0 and n == 0, stop=t == KT - 1 and n == 2)
                        last.then_inc(scores_ready, 1)
                        if has_pc(g0) and r == 0 and j in (1, 2):
                            transpose_chunk(j - 1)
                elif has_pc(g0) and r == 0:
                    transpose_chunk(0)
                    transpose_chunk(1)
                for n, c in enumerate(CHUNKS[r]):
                    if has_pc(g0):
                        if c + 2 < NC:
                            transpose_chunk(c + 2)
                        multiply_chunk(c)
                    if n == 0 and has_next_q(g0, r) and (s0 + 1) // 8 % 2 == 0:
                        if has_scores(g0):
                            pe.wait_ge(exp_done, s * NQ + 1)
                        make_q(s + 1, s0 + 1)
                    if n == 1 and has_next_q(g0, r):
                        if has_scores(g0):
                            pe.wait_ge(exp_done, s * NQ + 2)
                        make_qk(s + 1, s0 + 1)
                    if n == 2 and has_att(g0) and r == 0:
                        if g0 == 2:
                            pe.wait_ge(wvo_in, 32)
                        pe.wait_ge(pcT_ready, i * 4 + (g0 - 1))
                        if has_scores(g0):
                            pe.wait_ge(exp_done, s * NQ + NQ)
                        for m in range(4):
                            pair = 4 * (g0 % 2) + m
                            for e in range(2):
                                for t in range(KT):
                                    col = DH * (2 * pair + e)
                                    row = T * (2 * m + e)
                                    last = pe.matmul(ps_att[DH * e:DH * e + DH, T * m:T * m + T],
                                                     wv[:, t, col:col + DH], pcT[:, t, row:row + T],
                                                     start=t == 0, stop=t == KT - 1)
                        last.then_inc(att_ps, 1)
                    if n == 2 and has_out(g0) and r == 1:
                        pe.wait_ge(att_ready, i * 4 + (g0 - 1))
                        if has_scores(g0):
                            pe.wait_ge(exp_done, s * NQ + NQ)
                        for m in range(H // 2):
                            last = pe.matmul(ps_out, attT[:, m].rearrange("p b q -> p (b q)"), wo[:, m, :],
                                             start=m == 0, stop=m == H // 2 - 1)
                        last.then_inc(out_ps, 1)

            over_slots(pe, slot)


def self_attention_and_experts(nc, x1, x1_stats, alibi_d, WqkT, bqk, WV, bV, WoT, bo, gateT, gate_bias,
                               experts, ident_d, rank_d, diag_d, out):
    with ExitStack() as stack:
        def sb(name, shape, dt=F32):
            return stack.enter_context(nc.sbuf_tensor(name, shape, dt))

        def sem(name):
            return stack.enter_context(nc.semaphore(name))

        x1b = sb("x1b", [P, NT, D])
        x2 = sb("x2", [P, NT, D])
        xn = sb("xn", [P, NT, D])
        xnT = sb("xnT", [P, KT, TOK])
        wqk = sb("wqk", [P, KT, 4 * P])
        wvs = sb("wvs", [P, KT, 2 * P])
        woT = sb("woT", [P, KT, D])
        bqk_s = sb("bqk_s", [P, 4])
        bv = sb("bv", [P, P])
        bout = sb("bout", [P, D])
        alibi = sb("alibi", [P, H2 * T])
        ident = sb("ident2", [P, P])
        rank = sb("rank", [P, NE])
        diag = sb("diag", [P, 8])
        qkT = sb("qkT", [P, 4, TOK])
        kd = sb("kd", [P, 2, 2, 2, 8, T])
        vs = sb("vs", [P, NB, P])
        vd = sb("vd", [P, 2, 4, 5 * P])
        pr = sb("pr", [P, 3, H2, T])
        prT = sb("prT", [P, 2, 8, P])
        oT = sb("oT", [P, 2, KT, P])
        pmax = sb("pmax", [P, 3, 16])
        psum_r = sb("psum_r", [P, 3, 16])
        pinv = sb("pinv", [P, 3, 16])
        stats = sb("stats2", [P, NT, 6])
        mv = sb("mv2", [P, NT, 2])
        lnt = sb("lnt2", [P, 6, NT])
        xnT_hi = sb("xnT_hi", [P, KT, TOK], F32R)
        xnT_lo = sb("xnT_lo", [P, KT, TOK], F32R)
        gw = sb("gw", [P, KT, NE])
        gb = sb("gb", [P, NE])
        gt = pr[:, 0, 0:8, :].rearrange("p s (n e) -> p s n e", n=NT)
        gr = sb("gr", [P, 6, NT])
        gates = sb("gates", [P, NT, NX])
        w_raw = sb("w_raw", [P, 2, 6, D])
        w_hi = sb("w_hi", [P, 2, 6, D], F32R)
        w_lo = sb("w_lo", [P, 2, 6, D], F32R)
        act_a = qkT[:, 0].rearrange("p (m a) -> p m a", m=2)
        hid = qkT[:, 1].rearrange("p (m a) -> p m a", m=2)
        hid_hi = sb("hid_hi", [P, 2, KT, 512], F32R)
        hid_lo = sb("hid_lo", [P, 2, KT, 512], F32R)

        ps_a = stack.enter_context(nc.psum_tensor("ps_a", [P, 4, 512], F32))
        ps_b = stack.enter_context(nc.psum_tensor("ps_b", [P, 2, 512], F32))
        ps_c = stack.enter_context(nc.psum_tensor("ps_c", [P, 2, 512], F32))

        wv_in = sem("wv_in")
        wrest_in = sem("wrest_in")
        ew_in = [sem(f"ew_in{e}") for e in range(2)]
        chain_s = sem("dve_chain2")
        x1b_ready = sem("x1b_ready")
        var_ready = sem("var_ready2")
        root_ready = sem("root_ready2")
        xn_ready = sem("xn_ready2")
        xnT_ps = sem("xnT_ps")
        xnT_ready = sem("xnT_ready")
        wqk_in = sem("wqk_in")
        ident_in = sem("ident_in")
        qk_ps = sem("qk_ps2")
        qkT_ready = sem("qkT_ready")
        zeros_set = sem("zeros_set")
        kd_pool = sem("kd_pool")
        kd_dve = sem("kd_dve")
        vd_ready = sem("vd_ready")
        v_ps = sem("v_ps")
        v_ready = sem("v_ready")
        sc_ps = sem("sc_ps")
        sc_ready = sem("sc_ready")
        pmax_ready = sem("pmax_ready")
        shifted = sem("shifted")
        p_exp = sem("p_exp")
        psum_ready = sem("psum_ready")
        pinv_ready = sem("pinv_ready")
        p_ready = sem("p_ready")
        prT_ps = sem("prT_ps")
        prT_ready = sem("prT_ready")
        o_ps = sem("o_ps")
        oT_ready = sem("oT_ready")
        y_ps = sem("y_ps")
        x2_ready = sem("x2_ready")
        x2_stats_ready = sem("x2_stats_ready")
        xnT_hi_ready = sem("xnT_hi_ready")
        xnT_lo_ready = sem("xnT_lo_ready")
        gl_ps = sem("gl_ps")
        gl_shifted = sem("gl_shifted")
        gl_exp = sem("gl_exp")
        gates_ready = sem("gates_ready")
        ewh_ready = sem("ewh_ready")
        ew_ready = sem("ew_ready")
        ab2_ps = sem("ab2_ps")
        silu_ready = sem("silu_ready")
        hid_ready = sem("hid_ready")
        hid_hi_ready = sem("hid_hi_ready")
        hid_lo_ready = sem("hid_lo_ready")
        ey_ps = sem("ey_ps")
        acc_ready = sem("acc_ready")
        stored = sem("stored")
        ones_set = sem("ones_set")

        def wait(eng, s, count):
            if not isinstance(count, int) or count > 0:
                eng.wait_ge(s, count)

        block = stack.enter_context(nc.Block())

        def diagonal(eng, i, e):
            for o in range(2):
                k = qkT[:, 2 + o, T * (2 * i + e):T * (2 * i + e) + T]
                last = eng.tensor_tensor(kd[:, i % 2, e, o], k.unsqueeze(1).to_broadcast([P, 8, T]),
                                         diag[:].unsqueeze(2).to_broadcast([P, 8, T]), ALU.mult)
            return last

        @block.sync
        def _(sp):
            sp.dma_start(ident[:], ident_d).then_inc(ident_in, 16)
            sp.dma_start(wqk[:], WqkT.rearrange("(t p) n -> p t n", p=P)).then_inc(wqk_in, 16)
            sp.dma_start(bqk_s[:], bqk).then_inc(wqk_in, 16)
            sp.dma_start(wvs[:], WV.rearrange("(t p) n -> p t n", p=P)).then_inc(wv_in, 16)
            sp.dma_start(diag[:], diag_d).then_inc(wv_in, 16)
            for e in range(2):
                sp.dma_start(bv[T * e:T * e + T, :], bV[e].partition_broadcast(T)).then_inc(wv_in, 16)
            for e in range(2):
                sp.dma_start(alibi[T * e:T * e + T, :], alibi_d).then_inc(wv_in, 16)
            sp.dma_start(woT[:], WoT.rearrange("(t p) n -> p t n", p=P)).then_inc(wrest_in, 16)
            sp.dma_start(bout[:], bo.partition_broadcast(P)).then_inc(wrest_in, 16)
            sp.dma_start(gw[:], gateT.rearrange("(t p) n -> p t n", p=P)).then_inc(wrest_in, 16)
            sp.dma_start(gb[:], gate_bias.partition_broadcast(P)).then_inc(wrest_in, 16)
            sp.dma_start(rank[:], rank_d.partition_broadcast(P)).then_inc(wrest_in, 16)
            ew = experts.rearrange("x (w p) d -> x p w d", p=P)
            for e in range(2):
                sp.dma_start(w_raw[:, e], ew[e]).then_inc(ew_in[e], 16)
            with sp.Fori(0, NX // 2 - 1) as i:
                for e in range(2):
                    sp.wait_ge(ew_ready, i * 2 + (e + 1))
                    sp.dma_start(w_raw[:, e], ew[bass.ds(i * 2 + (2 + e), 1)].rearrange("x p w d -> p (x w) d")
                                 ).then_inc(ew_in[e], 16)
            outr = out.rearrange("(n p) d -> p n d", p=P)
            for h in range(2):
                for n in range(4):
                    sp.wait_ge(acc_ready, 8 * (NX - 1) + 4 * h + n + 1)
                    sp.dma_start(outr[:, 4 * h + n, :], x2[:, 4 * h + n, :]).then_inc(stored, 16)
            sp.wait_ge(stored, 16 * NT)

        @block.gpsimd
        def _(pool):
            pool.memset(gates[:, :, NE:NX], 1.0).then_inc(ones_set, 1)
            pool.memset(vd[:], 0.0).then_inc(zeros_set, 1)
            pool.wait_ge(wrest_in, 80)
            for n in range(NT):
                pool.tensor_tensor(x1b[:, n, :], x1[:, n, :], bout[:], ALU.add).then_inc(x1b_ready, 1)

            def diagonals(i):
                if i == 0:
                    pool.wait_ge(wv_in, 96)
                if i % 4 == 0:
                    pool.wait_ge(qkT_ready, i + 4)
                if i >= 2:
                    pool.wait_ge(sc_ps, i - 1)
                diagonal(pool, i, 0).then_inc(kd_pool, 1)

            def normalise(i):
                pool.wait_ge(pinv_ready, i + 1)
                pool.tensor_tensor(pr[:, i % 3], pr[:, i % 3], pinv[:, i % 3, :].unsqueeze(2).to_broadcast([P, 16, T]),
                                   ALU.mult).then_inc(p_ready, 1)

            def expert_weights(i, e):
                pool.wait_ge(ewh_ready, i * 2 + (e + 1))
                pool.tensor_tensor(w_lo[:, e % 2], w_raw[:, e % 2], w_hi[:, e % 2].bitcast(F32), ALU.subtract
                                   ).then_inc(ew_ready, 1)

            def split_xnT(m):
                t, cols = m % 2, slice(512 * (m // 2), 512 * (m // 2) + 512)
                pool.wait_ge(xnT_hi_ready, m + 1)
                pool.tensor_tensor(xnT_lo[:, t, cols], xnT[:, t, cols], xnT_hi[:, t, cols].bitcast(F32),
                                   ALU.subtract).then_inc(xnT_lo_ready, 1)

            diagonals(0)
            diagonals(1)
            for i in range(NT):
                pool.wait_ge(pmax_ready, i + 1)
                pool.tensor_tensor(pr[:, i % 3], pr[:, i % 3], pmax[:, i % 3, :].unsqueeze(2).to_broadcast([P, 16, T]),
                                   ALU.subtract).then_inc(shifted, 1)
                if i + 2 < NT:
                    diagonals(i + 2)
                if i >= 1:
                    normalise(i - 1)
                if i == NT - 2:
                    expert_weights(0, 0)
            normalise(NT - 1)
            for m in range(4):
                split_xnT(m)
            expert_weights(0, 1)
            with pool.Fori(1, NX // 2) as i:
                for e in range(2):
                    expert_weights(i, e)

        @block.scalar
        def _(act):
            def roots(n, cols):
                act.wait_ge(var_ready, n + 1)
                act.activation(lnt[:, 1, cols], lnt[:, 0, cols], ACT.Sqrt).then_inc(root_ready, 1)

            roots(0, slice(0, NT))
            act.wait_ge(wqk_in, 32)
            for n in range(8):
                act.wait_ge(qk_ps, n + 1)
                act.activation(qkT[:, n % 4, 512 * (n // 4):512 * (n // 4) + 512], ps_a[:, n % 4, :], ACT.Identity,
                               bias=bqk_s[:, n % 4:n % 4 + 1]).then_inc(qkT_ready, 1)

            def split_xnT(m):
                t, cols = m % 2, slice(512 * (m // 2), 512 * (m // 2) + 512)
                act.wait_ge(xnT_ready, 4 + m + 1)
                act.activation(xnT_hi[:, t, cols], xnT[:, t, cols], ACT.Copy).then_inc(xnT_hi_ready, 1)

            def split_weights(i, e):
                act.wait_ge(ew_in[e % 2], i * 16 + 16 * (e // 2 + 1))
                wait(act, ey_ps, i * 16 + 8 * (e - 1))
                act.activation(w_hi[:, e % 2], w_raw[:, e % 2], ACT.Copy).then_inc(ewh_ready, 1)

            def exp(i):
                act.wait_ge(shifted, i + 1)
                act.activation(pr[:, i % 3], pr[:, i % 3], ACT.Exp).then_inc(p_exp, 1)

            def take_oT(i):
                act.wait_ge(o_ps, i + 1)
                act.activation(oT[:, i % 2].rearrange("p t q -> p (t q)"), ps_c[:, i % 2, 0:KT * P], ACT.Copy
                               ).then_inc(oT_ready, 1)

            def take_prT(i):
                act.wait_ge(prT_ps, i + 1)
                act.activation(prT[:, i % 2].rearrange("p (a b) q -> p a (b q)", a=2), ps_b[:], ACT.Copy
                               ).then_inc(prT_ready, 1)

            def values(i):
                act.wait_ge(v_ready, i // 2 + 1)
                if i == 0:
                    act.wait_ge(zeros_set, 1)
                if i >= 2:
                    act.wait_ge(o_ps, i - 1)
                for o in range(2):
                    half = slice(T * o, T * o + T)
                    to = vd[half, i % 2].rearrange("p x (m c) -> p x m c", m=4)[:, :, :, DH2 * o:DH2 * o + DH2]
                    v = vs[half, 2 * i:2 * i + 2, :].rearrange("p e (w m c) -> p (e w) m c", w=2, m=4)
                    act.activation(to, v, ACT.Copy).then_inc(vd_ready, 1)

            split_weights(0, 0)
            for i in range(NT + 2):
                if i < NT:
                    exp(i)
                if i >= 2:
                    take_oT(i - 2)
                if 1 <= i <= NT:
                    take_prT(i - 1)
                if i < NT:
                    values(i)
                if i == NT - 2:
                    roots(1, slice(0, NT // 2))
                if i == NT:
                    split_xnT(0)
                    split_xnT(1)
            roots(2, slice(NT // 2, NT))

            def silu(i, e, h, m):
                act.wait_ge(ab2_ps, i * 8 + (4 * e + 2 * h + m + 1))
                act.activation(act_a[:, m, :], ps_a[:, 2 * m, :], ACT.Silu).then_inc(silu_ready, 1)

            def split_hidden(i, e, h, m):
                act.wait_ge(hid_ready, i * 8 + (4 * e + 2 * h + m + 1))
                act.activation(hid_hi[:, h, m, :], hid[:, m, :], ACT.Copy).then_inc(hid_hi_ready, 1)

            def hidden(i, e, h):
                wait(act, ey_ps, i * 16 + (8 * (e - 1) + 4 * h + 4))
                for m in range(KT):
                    silu(i, e, h, m)
                    split_hidden(i, e, h, m)

            def two_experts(i, last):
                for e in range(2):
                    if isinstance(i, int) and i == 0 and e == 0:
                        silu(0, 0, 0, 0)
                        split_hidden(0, 0, 0, 0)
                        silu(0, 0, 0, 1)
                        split_xnT(2)
                        split_xnT(3)
                        split_hidden(0, 0, 0, 1)
                        act.wait_ge(gl_shifted, 1)
                        act.activation(gt[:, 1], gt[:, 0], ACT.Exp).then_inc(gl_exp, 1)
                    else:
                        hidden(i, e, 0)
                    if not (last and e == 1):
                        split_weights(i, e + 1)
                    hidden(i, e, 1)

            two_experts(0, False)
            with act.Fori(1, NX // 2 - 1) as i:
                two_experts(i, False)
            two_experts(NX // 2 - 1, True)

        @block.vector
        def _(dve):
            chain = [0]

            def link(ins):
                chain[0] += 1
                ins.then_inc(chain_s, 1)
                dve.wait_ge(chain_s, chain[0])

            def layernorm(rows, tiles, st, k):
                cols = slice(tiles[0], tiles[-1] + 1)
                for n in tiles:
                    last = dve.bn_aggr(mv[:, n, :], st[:, n, :])
                link(last)
                dve.tensor_scalar(lnt[:, 0, cols], mv[:, cols, 1], EPS, None, ALU.add).then_inc(var_ready, 1)
                dve.wait_ge(var_ready, k + 1)
                dve.wait_ge(root_ready, k + 1)
                link(dve.reciprocal(lnt[:, 2, cols], lnt[:, 1, cols]))
                link(dve.tensor_tensor(lnt[:, 3, cols], lnt[:, 0, cols], lnt[:, 2, cols], ALU.mult))
                link(dve.tensor_tensor(lnt[:, 4, cols], lnt[:, 3, cols], lnt[:, 1, cols], ALU.add))
                link(dve.tensor_scalar(lnt[:, 5, cols], lnt[:, 4, cols], 0.5, None, ALU.mult))
                link(dve.reciprocal(lnt[:, 2, cols], lnt[:, 5, cols]))
                for n in tiles:
                    dve.tensor_scalar(xn[:, n, :], rows[:, n, :], mv[:, n, 0:1], lnt[:, 2, n:n + 1],
                                      ALU.subtract, ALU.mult).then_inc(xn_ready, 1)

            def take_xnT(k, h, ps):
                for t in range(KT):
                    dve.wait_ge(xnT_ps, 4 * k + 2 * h + t + 1)
                    dve.tensor_copy(xnT[:, t, 512 * h:512 * h + 512], ps[:, t, :]).then_inc(xnT_ready, 1)

            layernorm(x1, range(NT), x1_stats, 0)
            take_xnT(0, 0, ps_a[:, 0:2])
            take_xnT(0, 1, ps_a[:, 2:4])

            def diagonals(i):
                if i == 0:
                    dve.wait_ge(wv_in, 96)
                if i % 4 == 0:
                    dve.wait_ge(qkT_ready, i + 4)
                if i >= 2:
                    dve.wait_ge(sc_ps, i - 1)
                diagonal(dve, i, 1).then_inc(kd_dve, 1)

            def take_v(n):
                dve.wait_ge(v_ps, n + 1)
                dve.tensor_tensor(vs[:, 4 * n:4 * n + 4, :], ps_b[:, n % 2, :].rearrange("p (b c) -> p b c", b=4),
                                  bv[:].unsqueeze(1).to_broadcast([P, 4, P]), ALU.add).then_inc(v_ready, 1)

            def scores(i):
                s = pr[:, i % 3]
                dve.wait_ge(sc_ps, i + 1)
                if i >= 3:
                    dve.wait_ge(prT_ps, i - 2)
                dve.scalar_tensor_tensor(s.rearrange("p h k -> p (h k)"),
                                         ps_a[:, 2 * (i % 2):2 * (i % 2) + 2, :].rearrange("p w c -> p (w c)"),
                                         SCALE2, alibi[:], ALU.mult, ALU.add).then_inc(sc_ready, 1)
                dve.wait_ge(sc_ready, i + 1)
                dve.tensor_reduce(pmax[:, i % 3, :], s, AX.X, ALU.max).then_inc(pmax_ready, 1)

            def sums(i):
                dve.wait_ge(p_exp, i + 1)
                dve.tensor_reduce(psum_r[:, i % 3, :], pr[:, i % 3], AX.X, ALU.add).then_inc(psum_ready, 1)
                dve.wait_ge(psum_ready, i + 1)
                dve.reciprocal(pinv[:, i % 3, :], psum_r[:, i % 3, :]).then_inc(pinv_ready, 1)

            def residual(i):
                dve.wait_ge(x1b_ready, i + 1)
                dve.wait_ge(y_ps, i + 1)
                dve.tensor_tensor(x2[:, i, :], ps_c[:, i % 2, D:2 * D], x1b[:, i, :], ALU.add).then_inc(x2_ready, 1)
                dve.wait_ge(x2_ready, i + 1)
                dve.bn_stats(stats[:, i, :], x2[:, i, :]).then_inc(x2_stats_ready, 1)

            diagonals(0)
            diagonals(1)
            scores(0)
            diagonals(2)
            scores(1)
            take_v(0)
            for i in range(NT + 1):
                if i < NT:
                    sums(i)
                if i == 0:
                    for n in range(1, NB // 4):
                        take_v(n)
                if i + 3 < NT:
                    diagonals(i + 3)
                if i + 2 < NT:
                    scores(i + 2)
                if i == NT - 2:
                    dve.wait_ge(x2_stats_ready, NT // 2)
                    layernorm(x2, range(NT // 2), stats, 1)
                if i >= 1:
                    residual(i - 1)
                if i == NT - 1:
                    take_xnT(1, 0, ps_a[:, 0:2])
            dve.wait_ge(x2_stats_ready, NT)
            layernorm(x2, range(NT // 2, NT), stats, 2)

            def hidden_unit(i, e, h, m):
                unit = i * 8 + (4 * e + 2 * h + m)
                dve.wait_ge(silu_ready, unit + 1)
                dve.tensor_tensor(hid[:, m, :], act_a[:, m, :], ps_a[:, 2 * m + 1, :], ALU.mult
                                  ).then_inc(hid_ready, 1)
                dve.wait_ge(hid_hi_ready, unit + 1)
                dve.tensor_tensor(hid_lo[:, h, m, :], hid[:, m, :], hid_hi[:, h, m, :].bitcast(F32),
                                  ALU.subtract).then_inc(hid_lo_ready, 1)

            hidden_unit(0, 0, 0, 0)
            take_xnT(1, 1, ps_b)
            hidden_unit(0, 0, 0, 1)

            def over_e(a):
                return a.unsqueeze(2).to_broadcast([P, NT, NE])

            def over_n(a):
                return a.unsqueeze(1).to_broadcast([P, NT, NE])

            dve.wait_ge(gl_ps, 1)
            logits = ps_c[:, 0, 0:NT * NE].rearrange("p (n e) -> p n e", n=NT)
            link(dve.tensor_reduce(gr[:, 0, :], logits, AX.X, ALU.max))
            dve.tensor_tensor(gt[:, 0], logits, over_e(gr[:, 0, :]), ALU.subtract).then_inc(gl_shifted, 1)
            dve.wait_ge(gl_exp, 1)
            link(dve.tensor_reduce(gr[:, 1, :], gt[:, 1], AX.X, ALU.add))
            link(dve.reciprocal(gr[:, 2, :], gr[:, 1, :]))
            link(dve.tensor_tensor(gt[:, 2], gt[:, 1], over_e(gr[:, 2, :]), ALU.mult))
            dve.wait_ge(wrest_in, 80)
            link(dve.tensor_tensor(gt[:, 3], gt[:, 2], over_n(gb[:]), ALU.add))
            for k in range(2):
                biased, chosen = gt[:, 3], gt[:, 6 + k]
                link(dve.tensor_reduce(gr[:, 3, :], biased, AX.X, ALU.max))
                link(dve.tensor_tensor(gt[:, 4], biased, over_e(gr[:, 3, :]), ALU.is_ge))
                link(dve.tensor_tensor(gt[:, 5], gt[:, 4], over_n(rank[:]), ALU.mult))
                link(dve.tensor_reduce(gr[:, 4, :], gt[:, 5], AX.X, ALU.max))
                link(dve.tensor_tensor(chosen, gt[:, 5], over_e(gr[:, 4, :]), ALU.is_ge))
                if k == 0:
                    link(dve.scalar_tensor_tensor(biased, chosen, -BIG, biased, ALU.mult, ALU.add))
            link(dve.tensor_tensor(gt[:, 4], gt[:, 6], gt[:, 7], ALU.add))
            link(dve.tensor_tensor(gates[:, :, 0:NE], gt[:, 4], gt[:, 2], ALU.mult))

            def hidden(i, e, h):
                for m in range(KT):
                    hidden_unit(i, e, h, m)

            def accumulate(i, e, h):
                for n in range(4):
                    tile = 4 * h + n
                    dve.wait_ge(ey_ps, i * 16 + (8 * e + tile + 1))
                    wait(dve, acc_ready, i * 16 + (8 * e + tile + 1 - NT))
                    y = (ps_b, ps_c)[n // 2][:, n % 2, 0:D]
                    g = gates[:, tile, bass.ds(i * 2 + e, 1)]
                    dve.scalar_tensor_tensor(x2[:, tile, :], y, g, x2[:, tile, :], ALU.mult, ALU.add
                                             ).then_inc(acc_ready, 1)

            dve.wait_ge(ones_set, 1)
            hidden(0, 0, 1)
            accumulate(0, 0, 0)
            hidden(0, 1, 0)
            accumulate(0, 0, 1)
            hidden(0, 1, 1)
            accumulate(0, 1, 0)
            with dve.Fori(1, NX // 2) as i:
                hidden(i, 0, 0)
                accumulate(i - 1, 1, 1)
                hidden(i, 0, 1)
                accumulate(i, 0, 0)
                hidden(i, 1, 0)
                accumulate(i, 0, 1)
                hidden(i, 1, 1)
                accumulate(i, 1, 0)
            accumulate(NX // 2 - 1, 1, 1)

        @block.tensor
        def _(pe):
            pe.wait_ge(ident_in, 16)

            def transpose_xn(k, h, ps):
                for t in range(KT):
                    for n in range(4):
                        pe.wait_ge(xn_ready, NT * k + 4 * h + n + 1)
                        last = pe.transpose(ps[:, t, P * n:P * n + P], xn[:, 4 * h + n, P * t:P * t + P], ident[:])
                    last.then_inc(xnT_ps, 1)

            transpose_xn(0, 0, ps_a[:, 0:2])
            transpose_xn(0, 1, ps_a[:, 2:4])
            pe.wait_ge(wqk_in, 32)
            for n in range(8):
                if n in (0, 2):
                    pe.wait_ge(xnT_ready, n + 2)
                if n >= 4:
                    pe.wait_ge(qkT_ready, n - 3)
                for t in range(KT):
                    last = pe.matmul(ps_a[:, n % 4, :], wqk[:, t, P * (n % 4):P * (n % 4) + P],
                                     xnT[:, t, 512 * (n // 4):512 * (n // 4) + 512], start=t == 0, stop=t == KT - 1)
                last.then_inc(qk_ps, 1)

            def make_v(n):
                if n >= 2:
                    pe.wait_ge(v_ready, n - 1)
                for b in range(4 * n, 4 * n + 4):
                    for o in range(2):
                        for t in range(KT):
                            last = pe.matmul(ps_b[T * o:T * o + T, n % 2, P * (b % 4):P * (b % 4) + P],
                                             xnT[:, t, T * b:T * b + T], wvs[:, t, P * o:P * o + P],
                                             start=t == 0, stop=t == KT - 1)
                last.then_inc(v_ps, 1)

            def scores(i):
                pe.wait_ge(kd_pool, i + 1)
                pe.wait_ge(kd_dve, i + 1)
                if i < 2:
                    pe.wait_ge(qkT_ready, 6 + 2 * i)
                else:
                    pe.wait_ge(sc_ready, i - 1)
                for e in range(2):
                    tok = slice(T * (2 * i + e), T * (2 * i + e) + T)
                    for o in range(2):
                        last = pe.matmul(ps_a[T * e:T * e + T, 2 * (i % 2) + o, :], qkT[:, o, tok],
                                         kd[:, i % 2, e, o].rearrange("p h k -> p (h k)"), start=True, stop=True)
                last.then_inc(sc_ps, 1)

            def transpose_probs(i):
                pe.wait_ge(p_ready, i + 1)
                if i >= 1:
                    pe.wait_ge(prT_ready, i)
                else:
                    pe.wait_ge(v_ready, 4)
                for n in range(8):
                    last = pe.transpose(ps_b[:, n // 4, P * (n % 4):P * (n % 4) + P],
                                        pr[:, i % 3, 2 * n:2 * n + 2, :].rearrange("p h k -> p (h k)"), ident[:])
                last.then_inc(prT_ps, 1)

            def multiply_v(i):
                pe.wait_ge(prT_ready, i + 1)
                pe.wait_ge(vd_ready, 2 * i + 2)
                if i >= 2:
                    pe.wait_ge(x2_ready, i - 1)
                for e in range(2):
                    for w in range(2):
                        for m in range(4):
                            last = pe.matmul(ps_c[:, i % 2, P * w + T * e:P * w + T * e + T],
                                             vd[:, i % 2, 2 * e + w, P * m:P * m + P],
                                             prT[:, i % 2, 4 * w + m, T * e:T * e + T], start=m == 0, stop=m == 3)
                last.then_inc(o_ps, 1)

            def project(i):
                pe.wait_ge(oT_ready, i + 1)
                for t in range(KT):
                    last = pe.matmul(ps_c[:, i % 2, D:2 * D], oT[:, i % 2, t, :], woT[:, t, :], start=t == 0,
                                     stop=t == KT - 1)
                last.then_inc(y_ps, 1)

            pe.wait_ge(wv_in, 96)
            scores(0)
            scores(1)
            for n in range(NB // 4):
                make_v(n)
            pe.wait_ge(wrest_in, 80)
            for i in range(NT + 1):
                if i + 2 < NT:
                    scores(i + 2)
                if i == NT - 1:
                    pe.wait_ge(sc_ready, NT)
                    transpose_xn(1, 0, ps_a[:, 0:2])
                if i < NT:
                    transpose_probs(i)
                if i >= 1:
                    project(i - 1)
                if i < NT:
                    multiply_v(i)

            def router(tiles):
                for n in tiles:
                    for t in range(KT):
                        last = pe.matmul(ps_c[:, 0, NE * n:NE * n + NE], xnT[:, t, P * n:P * n + P], gw[:, t, :],
                                         start=t == 0, stop=t == KT - 1)
                return last

            def hidden(i, e, h):
                if h == 0:
                    pe.wait_ge(ew_ready, i * 2 + (e + 1))
                for m in range(KT):
                    unit = i * 8 + (4 * e + 2 * h + m)
                    wait(pe, hid_ready, unit - 1)
                    for k in range(2):
                        for t in range(KT):
                            parts = [(w_hi, xnT_hi), (w_lo, xnT_hi), (w_hi, xnT_lo)]
                            for n, (a, b) in enumerate(parts):
                                last = pe.matmul(ps_a[:, 2 * m + k, :], a[:, e, 2 * k + t, P * m:P * m + P],
                                                 b[:, t, 512 * h:512 * h + 512],
                                                 start=t == 0 and n == 0, stop=t == KT - 1 and n == 2)
                    last.then_inc(ab2_ps, 1)

            def outputs(i, e, h):
                unit = i * 8 + (4 * e + 2 * h)
                pe.wait_ge(hid_lo_ready, unit + 2)
                for n in range(4):
                    tile = 4 * h + n
                    wait(pe, acc_ready, i * 16 + (8 * e + tile + 1 - 4))
                    for t in range(KT):
                        parts = [(hid_hi, w_hi), (hid_lo, w_hi), (hid_hi, w_lo)]
                        for k, (a, b) in enumerate(parts):
                            last = pe.matmul((ps_b, ps_c)[n // 2][:, n % 2, 0:D], a[:, h, t, P * n:P * n + P],
                                             b[:, e, 4 + t, :], start=t == 0 and k == 0,
                                             stop=t == KT - 1 and k == 2)
                    last.then_inc(ey_ps, 1)

            pe.wait_ge(xnT_lo_ready, 2)
            hidden(0, 0, 0)
            transpose_xn(1, 1, ps_b)
            pe.wait_ge(x2_ready, NT - 1)
            router(range(NT // 2))
            pe.wait_ge(xnT_ready, 8)
            router(range(NT // 2, NT)).then_inc(gl_ps, 1)
            pe.wait_ge(xnT_lo_ready, 4)
            hidden(0, 0, 1)
            pe.wait_ge(gl_shifted, 1)
            outputs(0, 0, 0)
            hidden(0, 1, 0)
            outputs(0, 0, 1)
            hidden(0, 1, 1)
            outputs(0, 1, 0)
            with pe.Fori(1, NX // 2) as i:
                hidden(i, 0, 0)
                outputs(i - 1, 1, 1)
                hidden(i, 0, 1)
                outputs(i, 0, 0)
                hidden(i, 1, 0)
                outputs(i, 0, 1)
                hidden(i, 1, 1)
                outputs(i, 1, 0)
            outputs(NX // 2 - 1, 1, 1)


def program(nc, x, ctxT, ctx, Wq, WkT, Wv, Wo, alibi, WqkT, bqk, WV, bV, WoT, bo, gateT, gate_bias,
            experts, ident, rank, diag, out):
    with nc.sbuf_tensor("x1", [P, NT, D], F32) as x1, nc.sbuf_tensor("x1_stats", [P, NT, 6], F32) as x1_stats:
        cross_attention(nc, x, ctxT, ctx, Wq, WkT, Wv, Wo, ident, x1, x1_stats)
        self_attention_and_experts(nc, x1, x1_stats, alibi, WqkT, bqk, WV, bV, WoT, bo, gateT, gate_bias,
                                   experts, ident, rank, diag, out)


def layouts(v):
    qkv = v["L0_attn_qkv_w"].reshape(H2, 3 * DH2, D)
    qkv_b = v["L0_attn_qkv_b"].reshape(H2, 3 * DH2)

    def even_odd(a):
        return a.reshape(2, 4, 2, *a.shape[1:]).transpose(2, 0, 1, *range(3, a.ndim + 2))

    pos = np.arange(T, dtype=np.float32)
    slopes = np.float32(0.5) ** np.arange(H2, dtype=np.float32)
    dist = -np.abs(pos[:, None] - pos[None, :])[:, None, :] * slopes[None, :, None]
    return {
        "x": v["x"].reshape(TOK, D),
        "ctxT": v["ctx_1024"].transpose(0, 2, 1),
        "ctx": v["ctx_1024"],
        "Wq": v["L0_xattn_Wq"],
        "WkT": v["L0_xattn_Wk"].T,
        "Wv": v["L0_xattn_Wv"],
        "Wo": v["L0_xattn_Wo"],
        "alibi": dist.reshape(T, H2 * T),
        "WqkT": qkv[:, 0:2 * DH2].reshape(H2, 2, DH2, D).transpose(1, 0, 2, 3).reshape(4 * P, D).T,
        "bqk": qkv_b[:, 0:2 * DH2].reshape(H2, 2, DH2).transpose(1, 0, 2).reshape(4, P).T,
        "WV": even_odd(qkv[:, 2 * DH2:]).reshape(D, D).T,
        "bV": even_odd(qkv_b[:, 2 * DH2:]).reshape(2, P),
        "WoT": v["L0_attn_out_w"].T,
        "bo": v["L0_attn_out_b"],
        "gateT": v["L0_ffn_gate_w"].T,
        "gate_bias": v["L0_ffn_gate_bias"],
        "experts": np.concatenate([
            np.concatenate([v["L0_ffn_w1"].transpose(0, 2, 1), v["L0_ffn_w3"].transpose(0, 2, 1),
                            v["L0_ffn_w2"].transpose(0, 2, 1)], axis=1),
            np.concatenate([v["L0_ffn_sw1"].reshape(NSH, INTER, D).transpose(0, 2, 1),
                            v["L0_ffn_sw3"].reshape(NSH, INTER, D).transpose(0, 2, 1),
                            v["L0_ffn_sw2"].T.reshape(NSH, INTER, D)], axis=1)], axis=0),
        "ident": np.eye(P, dtype=np.float32),
        "rank": np.arange(NE, 0, -1, dtype=np.float32),
        "diag": np.repeat(np.eye(8, dtype=np.float32), DH2, axis=0),
    }


def kernel(**inputs):
    import numpy as _np
    import concourse.bacc as _bacc
    from concourse import mybir as _mybir
    from concourse.bass_utils import run_bass_kernel_spmd as _run

    nc = _bacc.Bacc("TRN2", target_bir_lowering=False, num_devices=1)
    arrays, args = {}, {}
    for name, a in layouts({k: _np.asarray(v) for k, v in inputs.items()}).items():
        a = _np.ascontiguousarray(a)
        arrays[f"in_{name}_dram"] = a
        args[name] = nc.dram_tensor(f"in_{name}_dram", a.shape, _mybir.dt.from_np(a.dtype), kind="ExternalInput").ap()
    out = nc.dram_tensor("out_0_dram", (TOK, D), _mybir.dt.float32, kind="ExternalOutput").ap()
    program(nc, out=out, **args)
    r = _run(nc, [arrays], core_ids=[0])
    return r.results[0]["out_0_dram"].reshape(NB, T, D)
```

```python
from contextlib import ExitStack

import numpy as np

import concourse.bass as bass
from concourse import mybir

ALU = mybir.AluOpType
ACT = mybir.ActivationFunctionType
AX = mybir.AxisListType
F32 = mybir.dt.float32
F32R = mybir.dt.float32r

P = 128
NB, T, D, S = 16, 64, 256, 1601
H, DH = 16, 64
KT = D // P
TOK = NB * T
NT = TOK // P
NG = 2
NR = 4
NQ = 4
QW = 400
SP = 1602
QE = [QW, QW, QW, SP - 3 * QW]
QV = [QW, QW, QW, S - 3 * QW]
NC = -(-S // P)
CW = [P] * (NC - 1) + [S - (NC - 1) * P]
CHUNKS = [range(0, 3), range(3, 6), range(6, 9), range(9, 13)]
ALL_GROUPS = NB * NG
SCALE = DH ** -0.5
EPS = 1e-5
H2, DH2 = 16, 16
SCALE2 = DH2 ** -0.5
NE, NSH, INTER = 8, 2, 256
NX = NE + NSH
BIG = 1e30


def cross_attention(nc, x, ctxT, ctx, Wq, WkT, Wv, Wo, ident_d, ident, x1, stats, mv, lnt):
    with ExitStack() as stack:
        def sb(name, shape, dt=F32):
            return stack.enter_context(nc.sbuf_tensor(name, shape, dt))

        def sem(name):
            return stack.enter_context(nc.semaphore(name))

        probs = sb("probs", [P, 2, NR, SP])
        pT_hi = sb("pT_hi", [P, 4, NR * P], F32R)
        pT_lo = sb("pT_lo", [P, 4, NR * P], F32R)
        ctx_raw = sb("ctx_raw", [P, NC, D])
        ctx_hi = sb("ctx_hi", [P, NC, D], F32R)
        ctx_lo = sb("ctx_lo", [P, NC, D], F32R)
        ctxT_raw = sb("ctxT_raw", [P, KT, SP])
        ctxT_hi = sb("ctxT_hi", [P, KT, SP], F32R)
        ctxT_lo = sb("ctxT_lo", [P, KT, SP], F32R)
        xT = sb("xT", [P, KT, TOK])
        wq = sb("wq", [P, KT, H * DH])
        wkT = sb("wkT", [P, H // 2, D])
        wv = sb("wv", [P, KT, H * DH])
        wo = sb("wo", [P, H // 2, D])
        qT = sb("qT", [P, 2, T])
        qT_odd = sb("qT_odd", [P, H // 2, T])
        qk_hi = sb("qk_hi", [P, KT, P], F32R)
        qk_lo = sb("qk_lo", [P, KT, P], F32R)
        pcT = sb("pcT", [P, KT, NR * P])
        attT = sb("attT", [P, H // 2, 2, T])
        ones = sb("ones", [P, 1])
        bmax = sb("bmax", [P, 2, NQ])
        nmax = sb("nmax", [P, 2])
        psums = sb("psums", [P, 2, NQ])
        rsum = sb("rsum", [P, 2])
        rinv = sb("rinv", [P, 2])
        x_tile = sb("x_tile", [P, D])
        x_rows = probs[:, 1, 0:2, :].rearrange("p a b -> p (a b)")[:, 0:NT * D].rearrange(
            "p (n d) -> p n d", n=NT)

        ps_s = stack.enter_context(nc.psum_tensor("ps_s", [P, NQ, 512], F32))
        ps_t = stack.enter_context(nc.psum_tensor("ps_t", [P, 2, 512], F32))
        ps_o = stack.enter_context(nc.psum_tensor("ps_o", [P, KT, 512], F32))

        x_in = [sem("x_first_in"), sem("x_rest_in")]
        w_in = [sem("w_first_in"), sem("w_rest_in")]
        ident_in = sem("ident_in")
        first_ctxT_in = [sem(f"first_ctxT_in{j}") for j in range(NQ)]
        wvo_in = sem("wvo_in")
        ctxT_in = sem("ctxT_in")
        ctx_in = sem("ctx_in")
        ctx_tail_in = sem("ctx_tail_in")
        pad_set = sem("pad_set")
        ln_chain = sem("ln_chain")
        ln_var = sem("ln_var")
        ln_root = sem("ln_root")
        xn_ready = sem("xn_ready")
        xt_ps = sem("xt_ps")
        xT_ready = sem("xT_ready")
        ctxT_hi_ready = sem("ctxT_hi_ready")
        ctxT_ready = sem("ctxT_ready")
        ctx_hi_ready = sem("ctx_hi_ready")
        ctx_ready = sem("ctx_ready")
        scores_ready = sem("scores_ready")
        bmax_ready = sem("bmax_ready")
        nmax_ready = sem("nmax_ready")
        exp_done = sem("exp_done")
        rsum_ready = sem("rsum_ready")
        rinv_ready = sem("rinv_ready")
        probs_ready = sem("probs_ready")
        pT_ps = sem("pT_ps")
        pT_hi_ready = sem("pT_hi_ready")
        pT_ready = sem("pT_ready")
        pc_done = sem("pc_done")
        pcT_ready = sem("pcT_ready")
        q_ps = sem("q_ps")
        q_ready = sem("q_ready")
        qk_ps = sem("qk_ps")
        qk_hi_ready = sem("qk_hi_ready")
        qk_ready = sem("qk_ready")
        att_ps = sem("att_ps")
        att_ready = sem("att_ready")
        out_ps = sem("out_ps")
        out_ready = sem("out_ready")
        x_tile_in = sem("x_tile_in")
        x1_stats_ready = sem("x1_stats_ready")

        def wait(eng, s, count):
            if not isinstance(count, int) or count > 0:
                eng.wait_ge(s, count)

        def over_slots(eng, slot):
            for g0 in range(2):
                for r in range(NR):
                    slot(0, g0, r)
            with eng.Fori(0, ALL_GROUPS // 4 - 1) as i:
                for g0 in range(2, 6):
                    for r in range(NR):
                        slot(i, g0, r)
            for g0 in range(ALL_GROUPS - 2, ALL_GROUPS + 2):
                for r in range(NR):
                    slot(0, g0, r)

        def has_scores(g0):
            return g0 < ALL_GROUPS

        def has_pc(g0):
            return 1 <= g0 <= ALL_GROUPS

        def has_att(g0):
            return g0 >= 2

        def has_out(g0):
            return g0 >= 5 and g0 % 4 == 1

        def has_next_q(g0, r):
            return 4 * g0 + r + 1 < 4 * ALL_GROUPS

        def keys(j):
            return slice(QW * j, QW * j + QE[j])

        def ps_q_of(n0):
            return (ps_o if n0 <= NR else ps_s)[:, 0, 0:2 * T]

        def ps_qk_of(n0):
            return (ps_o if n0 <= NR else ps_s)[:, 1, 0:KT * P]

        ps_att = ps_s[:, 3, 0:4 * T]
        ps_out = ps_s[:, 3, 256:256 + D]

        xT_rest = ps_t[:].rearrange("p a b -> p (a b)")[:, 0:TOK - P]

        def q_jobs(i, n0):
            return i * 8 + (n0 // 16 * 8 + min(n0 % 16, 7) + 1)

        x_tiles = x.rearrange("(n p) d -> p n d", p=P)
        block = stack.enter_context(nc.Block())

        @block.sync
        def _(sp):
            ctxT_v = ctxT.rearrange("b (t p) s -> b p t s", p=P)
            ctx_v = ctx[:, 0:(NC - 1) * P, :].rearrange("b (c p) d -> b p c d", p=P)
            wq_v = Wq.rearrange("(t p) n -> p t n", p=P)
            wkT_v = WkT.rearrange("(t p) n -> p t n", p=P)
            sp.dma_start(x_rows[:, 0:1, :], x_tiles[:, 0:1, :]).then_inc(x_in[0], 16)
            sp.dma_start(ident[:], ident_d).then_inc(ident_in, 16)
            sp.dma_start(wq[:, :, 0:2 * P], wq_v[:, :, 0:2 * P]).then_inc(w_in[0], 16)
            sp.dma_start(wkT[:, 0:2, :], wkT_v[:, 0:2, :]).then_inc(w_in[0], 16)
            for j in range(NQ):
                cols = slice(QW * j, QW * j + QV[j])
                sp.dma_start(ctxT_raw[:, :, cols], ctxT_v[0][:, :, cols]).then_inc(first_ctxT_in[j], 16)
            sp.dma_start(x_rows[:, 1:NT, :], x_tiles[:, 1:NT, :]).then_inc(x_in[1], 16)
            sp.dma_start(wq[:, :, 2 * P:], wq_v[:, :, 2 * P:]).then_inc(w_in[1], 16)
            sp.dma_start(wkT[:, 2:, :], wkT_v[:, 2:, :]).then_inc(w_in[1], 16)
            sp.dma_start(ctx_raw[:, 0:NC - 1, :], ctx_v[0]).then_inc(ctx_in, 16)
            sp.dma_start(ctx_raw[0:CW[-1], NC - 1, :], ctx[0, (NC - 1) * P:S, :]).then_inc(ctx_tail_in, 16)
            sp.dma_start(wv[:], Wv.rearrange("(t p) n -> p t n", p=P)).then_inc(wvo_in, 16)
            sp.dma_start(wo[:], Wo.rearrange("(t p) n -> p t n", p=P)).then_inc(wvo_in, 16)
            with sp.Fori(0, NB - 1) as b:
                sp.wait_ge(ctxT_ready, b * NQ + NQ)
                sp.dma_start(ctxT_raw[:, :, 0:S], ctxT_v[bass.ds(b + 1, 1)].rearrange("b p t s -> p (b t) s")
                             ).then_inc(ctxT_in, 16)
                sp.wait_ge(ctx_ready, b * NC + NC)
                sp.dma_start(ctx_raw[:, 0:NC - 1, :], ctx_v[bass.ds(b + 1, 1)].rearrange("b p c d -> p (b c) d")
                             ).then_inc(ctx_in, 16)
                sp.dma_start(ctx_raw[0:CW[-1], NC - 1, :],
                             ctx[bass.ds(b + 1, 1), (NC - 1) * P:S, :].rearrange("b p d -> (b p) d")
                             ).then_inc(ctx_tail_in, 16)

        @block.gpsimd
        def _(pool):
            pool.memset(ctxT_raw[:, :, S:SP], 0.0).then_inc(pad_set, 1)
            pool.memset(ones[:], 1.0).then_inc(pad_set, 1)
            pool.wait_ge(pad_set, 2)

            def split_ctxT(b):
                for j in range(NQ):
                    pool.wait_ge(ctxT_hi_ready, b * NQ + j + 1)
                    pool.tensor_tensor(ctxT_lo[:, :, keys(j)], ctxT_raw[:, :, keys(j)],
                                       ctxT_hi[:, :, keys(j)].bitcast(F32), ALU.subtract).then_inc(ctxT_ready, 1)

            def split_ctx(b):
                pool.wait_ge(ctx_in, b * 16 + 16)
                pool.wait_ge(ctx_tail_in, b * 16 + 16)
                for c in range(NC):
                    w = CW[c]
                    if not (isinstance(b, int) and b == 0):
                        pool.wait_ge(pc_done, b * (NG * NC) + (c + 1 - NC))
                    pool.tensor_tensor(ctx_hi[0:w, c, :], ctx_raw[0:w, c, :], ones[0:w, :].to_broadcast([w, D]),
                                       ALU.mult).then_inc(ctx_hi_ready, 1)
                    pool.wait_ge(ctx_hi_ready, b * NC + c + 1)
                    pool.tensor_tensor(ctx_lo[0:w, c, :], ctx_raw[0:w, c, :], ctx_hi[0:w, c, :].bitcast(F32),
                                       ALU.subtract).then_inc(ctx_ready, 1)

            split_ctxT(0)
            split_ctx(0)
            with pool.Fori(0, NB - 1) as b:
                split_ctxT(b + 1)
                split_ctx(b + 1)

        @block.scalar
        def _(act):
            def roots(k, tiles):
                act.wait_ge(ln_var, k + 1)
                act.activation(lnt[:, 1, tiles], lnt[:, 0, tiles], ACT.Sqrt).then_inc(ln_root, 1)

            roots(0, slice(0, 1))

            def split_ctxT(b, j):
                if isinstance(b, int) and b == 0:
                    act.wait_ge(first_ctxT_in[j], 16)
                else:
                    act.wait_ge(ctxT_in, b * 16)
                act.activation(ctxT_hi[:, :, keys(j)], ctxT_raw[:, :, keys(j)], ACT.Copy
                               ).then_inc(ctxT_hi_ready, 1)

            act.wait_ge(pad_set, 1)
            for j in range(NQ):
                split_ctxT(0, j)

            def take_qk(n, ps_qk):
                if isinstance(n, int) and 1 <= n <= NR:
                    act.wait_ge(scores_ready, n * NQ)
                act.wait_ge(qk_ps, n + 1)
                act.activation(qk_hi[:].rearrange("p t q -> p (t q)"), ps_qk, ACT.Copy, scale=SCALE
                               ).then_inc(qk_hi_ready, 1)

            take_qk(0, ps_qk_of(0))

            def slot(i, g0, r):
                g, s = i * 4 + g0, i * 16 + (4 * g0 + r)
                chunk = i * (4 * NC) + NC * (g0 - 1)

                def take_pT(c):
                    w = CW[c]
                    act.wait_ge(pT_ps, chunk + c + 1)
                    wait(act, pc_done, chunk + c + 1 - 4)
                    act.activation(pT_hi[0:w, (NC * (g0 - 1) + c) % 4, :], ps_t[0:w, (NC * (g0 - 1) + c) % 2, :],
                                   ACT.Copy).then_inc(pT_hi_ready, 1)

                def exp(j):
                    if j == 0:
                        act.wait_ge(nmax_ready, s + 1)
                        wait(act, pT_ps, chunk)
                    act.activation(probs[:, g0 % 2, r, QW * j:QW * j + QV[j]], ps_s[:, j, 0:QV[j]], ACT.Exp,
                                   bias=nmax[:, s0 % 2:s0 % 2 + 1],
                                   accum_out=psums[:, s0 % 2, j:j + 1]).then_inc(exp_done, 1)

                s0 = 4 * g0 + r
                if has_out(g0) and r == 0:
                    wait(act, out_ready, i + (g0 - 5) // 4)
                    act.dma_start(x_tile[:].unsqueeze(1), x_tiles[:, bass.ds(i + (g0 - 5) // 4, 1), :]
                                  ).then_inc(x_tile_in, 16)
                if has_pc(g0) and r == 0:
                    take_pT(0)
                    take_pT(1)
                if g0 % 2 == 1 and r == 3 and g0 < ALL_GROUPS - 1:
                    for j in range(NQ):
                        act.wait_ge(scores_ready, s * NQ + j + 1)
                        split_ctxT(i * 2 + (g0 // 2 + 1), j)
                if g0 == 0:
                    take_qk(s + 1, ps_qk_of(s0 + 1))
                for n, c in enumerate(CHUNKS[r]):
                    if has_scores(g0):
                        for j in ([0], [1, 2], [3], [])[n]:
                            exp(j)
                    if n == 2 and has_next_q(g0, r) and has_pc(g0):
                        take_qk(s + 1, ps_qk_of(s0 + 1))
                    if has_pc(g0) and c + 2 < NC:
                        take_pT(c + 2)
                if g0 == 0 and r == 0:
                    roots(1, slice(1, NT))
                if g0 == ALL_GROUPS and r == NR - 1:
                    roots(2, slice(0, NT - 1))

            over_slots(act, slot)

        @block.vector
        def _(dve):
            chain = [0]

            def link(ins):
                chain[0] += 1
                ins.then_inc(ln_chain, 1)
                dve.wait_ge(ln_chain, chain[0])

            link(dve.memset(qT[:], 0.0))

            def variances(k, tiles):
                dve.wait_ge(x_in[k], 16)
                for n in tiles:
                    last = dve.bn_stats(stats[:, n, :], x_rows[:, n, :])
                link(last)
                means(tiles)

            def means(tiles):
                cols = slice(tiles[0], tiles[-1] + 1)
                for n in tiles:
                    last = dve.bn_aggr(mv[:, n, :], stats[:, n, :])
                link(last)
                dve.tensor_scalar(lnt[:, 0, cols], mv[:, cols, 1], EPS, None, ALU.add).then_inc(ln_var, 1)

            def inverse_roots(k, tiles):
                cols = slice(tiles[0], tiles[-1] + 1)
                dve.wait_ge(ln_var, k + 1)
                dve.wait_ge(ln_root, k + 1)
                link(dve.reciprocal(lnt[:, 2, cols], lnt[:, 1, cols]))
                link(dve.tensor_tensor(lnt[:, 3, cols], lnt[:, 0, cols], lnt[:, 2, cols], ALU.mult))
                link(dve.tensor_tensor(lnt[:, 4, cols], lnt[:, 3, cols], lnt[:, 1, cols], ALU.add))
                link(dve.tensor_scalar(lnt[:, 5, cols], lnt[:, 4, cols], 0.5, None, ALU.mult))
                link(dve.reciprocal(lnt[:, 2, cols], lnt[:, 5, cols]))

            def normalise(tiles):
                for n in tiles:
                    dve.tensor_scalar(x_rows[:, n, :], x_rows[:, n, :], mv[:, n, 0:1], lnt[:, 2, n:n + 1],
                                      ALU.subtract, ALU.mult).then_inc(xn_ready, 1)

            variances(0, range(1))
            inverse_roots(0, range(1))
            normalise(range(1))
            dve.wait_ge(xt_ps, 1)
            dve.tensor_copy(xT[:, :, 0:P], ps_s[:, 0, 0:KT * P].rearrange("p (t q) -> p t q", t=KT)
                            ).then_inc(xT_ready, 1)

            def take_xT(t):
                dve.wait_ge(xt_ps, t + 2)
                dve.tensor_copy(xT[:, t, P:TOK], xT_rest).then_inc(xT_ready, 1)

            def take_q(i, n, n0):
                ps_q = ps_q_of(n0)
                if n0 // 8 % 2 == 0:
                    dve.wait_ge(q_ps, q_jobs(i, n0))
                    dve.tensor_copy(qT_odd[:, n0 % 8, :], ps_q[:, T:2 * T])
                    src = ps_q[:, 0:T]
                else:
                    dve.wait_ge(q_ready, n - 7)
                    dve.wait_ge(qk_ps, n)
                    src = qT_odd[:, n0 % 8, :]
                dve.tensor_copy(qT[0:DH, 0, :], src[0:DH])
                dve.tensor_copy(qT[DH:P, 1, :], src[DH:P]).then_inc(q_ready, 1)

            def take_qk(n, ps_qk):
                dve.wait_ge(qk_hi_ready, n + 1)
                lo, hi = (a[:].rearrange("p t q -> p (t q)") for a in (qk_lo, qk_hi))
                dve.scalar_tensor_tensor(lo, ps_qk, SCALE, hi.bitcast(F32), ALU.mult, ALU.subtract
                                         ).then_inc(qk_ready, 1)

            take_q(0, 0, 0)
            take_qk(0, ps_qk_of(0))
            take_q(0, 1, 1)

            def slot(i, g0, r):
                s, s0 = i * 16 + (4 * g0 + r), 4 * g0 + r
                chunk = i * (4 * NC) + NC * (g0 - 1)

                def take_pT(c):
                    w, at = CW[c], NC * (g0 - 1) + c
                    dve.wait_ge(pT_hi_ready, chunk + c + 1)
                    dve.tensor_tensor(pT_lo[0:w, at % 4, :], ps_t[0:w, at % 2, :],
                                      pT_hi[0:w, at % 4, :].bitcast(F32), ALU.subtract).then_inc(pT_ready, 1)

                if has_att(g0) and r == 0:
                    dve.wait_ge(pc_done, chunk)
                    dve.tensor_copy(pcT[:], ps_o[:]).then_inc(pcT_ready, 1)
                if g0 == 0 and r == NR - 1:
                    take_xT(0)
                if has_scores(g0):
                    for j in range(NQ):
                        dve.wait_ge(scores_ready, s * NQ + j + 1)
                        dve.tensor_reduce(bmax[:, s0 % 2, j:j + 1], ps_s[:, j, 0:QV[j]], AX.X, ALU.max
                                          ).then_inc(bmax_ready, 1)
                        if has_pc(g0) and r == 0 and j == 2:
                            take_pT(0)
                    dve.wait_ge(bmax_ready, s * NQ + NQ)
                    dve.tensor_reduce(nmax[:, s0 % 2:s0 % 2 + 1], bmax[:, s0 % 2, :], AX.X, ALU.max, negate=True
                                      ).then_inc(nmax_ready, 1)
                    if g0 == 0:
                        take_qk(s + 1, ps_qk_of(s0 + 1))
                        if r == 0:
                            variances(1, range(1, NT))
                        elif r == 1:
                            inverse_roots(1, range(1, NT))
                            normalise(range(1, 3))
                        elif r == 2:
                            normalise(range(3, NT))
                        else:
                            take_xT(1)
                    if has_pc(g0) and r == 0:
                        take_pT(1)
                elif has_pc(g0) and r == 0:
                    take_pT(0)
                    take_pT(1)
                for n, c in enumerate(CHUNKS[r]):
                    if n == 2 and has_next_q(g0, r) and g0 > 0:
                        take_qk(s + 1, ps_qk_of(s0 + 1))
                    if has_pc(g0) and c + 2 < NC:
                        take_pT(c + 2)
                    if n == 0 and has_next_q(g0, r) and g0 > 0:
                        take_q(i, s + 1, s0 + 1)
                if g0 == ALL_GROUPS and r == NR - 1:
                    dve.wait_ge(x1_stats_ready, NT - 1)
                    means(range(NT - 1))
                    inverse_roots(2, range(NT - 1))
                if has_att(g0) and r == 0:
                    dve.wait_ge(att_ps, i * 4 + (g0 - 1))
                    dve.tensor_copy(attT[:, 4 * (g0 % 2):4 * (g0 % 2) + 4, (g0 - 2) // 2 % 2, :],
                                    ps_att.rearrange("p (m q) -> p m q", m=4)).then_inc(att_ready, 1)
                if has_out(g0) and r == 1:
                    dve.wait_ge(out_ps, i + (g0 - 1) // 4)
                    dve.wait_ge(x_tile_in, i * 16 + 16 * ((g0 - 1) // 4))
                    tile = bass.ds(i + (g0 - 5) // 4, 1)
                    dve.tensor_tensor(x1[:, tile, :], ps_out.unsqueeze(1), x_tile[:].unsqueeze(1), ALU.add
                                      ).then_inc(out_ready, 1)
                    dve.wait_ge(out_ready, i + (g0 - 1) // 4)
                    dve.bn_stats(stats[:, tile, :], x1[:, tile, :]).then_inc(x1_stats_ready, 1)
                if has_scores(g0):
                    dve.wait_ge(exp_done, s * NQ + NQ)
                    dve.tensor_reduce(rsum[:, s0 % 2:s0 % 2 + 1], psums[:, s0 % 2, :], AX.X, ALU.add
                                      ).then_inc(rsum_ready, 1)
                    dve.wait_ge(rsum_ready, s + 1)
                    dve.reciprocal(rinv[:, s0 % 2:s0 % 2 + 1], rsum[:, s0 % 2:s0 % 2 + 1]).then_inc(rinv_ready, 1)
                    if g0 == 0 and r < NR - 1:
                        take_q(i, s + 2, s0 + 2)
                    dve.wait_ge(rinv_ready, s + 1)
                    dve.tensor_scalar(probs[:, g0 % 2, r, 0:S], probs[:, g0 % 2, r, 0:S],
                                      rinv[:, s0 % 2:s0 % 2 + 1], None, ALU.mult).then_inc(probs_ready, 1)

            over_slots(dve, slot)

        @block.tensor
        def _(pe):
            pe.wait_ge(ident_in, 16)
            pe.wait_ge(xn_ready, 1)
            for t in range(KT):
                last = pe.transpose(ps_s[:, 0, P * t:P * t + P], x_rows[:, 0, P * t:P * t + P], ident[:])
            last.then_inc(xt_ps, 1)

            def transpose_x(t):
                wait(pe, xT_ready, t + 1)
                for n in range(1, NT):
                    pe.wait_ge(xn_ready, n + 1)
                    last = pe.transpose(xT_rest[:, P * (n - 1):P * n], x_rows[:, n, P * t:P * t + P], ident[:])
                last.then_inc(xt_ps, 1)

            def make_q(n, n0):
                tok = bass.ds((n - n0 % 8) * (T // 8), 2 * T)
                for t in range(KT):
                    last = pe.matmul(ps_q_of(n0), wq[:, t, P * (n0 % 8):P * (n0 % 8) + P], xT[:, t, tok],
                                     start=t == 0, stop=t == KT - 1)
                last.then_inc(q_ps, 1)

            def make_qk(n, n0):
                pe.wait_ge(q_ready, n + 1)
                for t in range(KT):
                    last = pe.matmul(ps_qk_of(n0)[:, P * t:P * t + P], wkT[:, n0 % 8, P * t:P * t + P],
                                     qT[:].rearrange("p e q -> p (e q)"), start=True, stop=True)
                last.then_inc(qk_ps, 1)

            pe.wait_ge(xT_ready, 1)
            pe.wait_ge(w_in[0], 32)
            make_q(0, 0)
            make_qk(0, 0)

            def slot(i, g0, r):
                s, s0 = i * 16 + (4 * g0 + r), 4 * g0 + r
                chunk, chunk0 = i * (4 * NC) + NC * (g0 - 1), NC * (g0 - 1)

                def transpose_chunk(c):
                    w = CW[c]
                    if c == 0:
                        pe.wait_ge(probs_ready, i * 16 + 4 * g0)
                    wait(pe, pT_ready, chunk + c - 1)
                    for n in range(NR):
                        last = pe.transpose(ps_t[0:w, (chunk0 + c) % 2, P * n:P * n + P],
                                            probs[:, (g0 - 1) % 2, n, P * c:P * c + w], ident[:])
                    last.then_inc(pT_ps, 1)

                def multiply_chunk(c):
                    w, at = CW[c], (chunk0 + c) % 4
                    if c == 0:
                        wait(pe, pcT_ready, i * 4 + (g0 - 1))
                    if g0 % 2 == 1:
                        pe.wait_ge(ctx_ready, i * (2 * NC) + (g0 // 2 * NC + c + 1))
                    pe.wait_ge(pT_ready, chunk + c + 1)
                    for t in range(KT):
                        parts = [(ctx_hi, pT_hi), (ctx_lo, pT_hi), (ctx_hi, pT_lo)]
                        for n, (a, b) in enumerate(parts):
                            last = pe.matmul(ps_o[:, t, :], a[0:w, c, P * t:P * t + P], b[0:w, at, :],
                                             start=c == 0 and n == 0, stop=c == NC - 1 and n == 2)
                    last.then_inc(pc_done, 1)

                if has_scores(g0):
                    if g0 == 0 and r == 1:
                        pe.wait_ge(w_in[1], 32)
                    if g0 == 1 and r == 0:
                        pe.wait_ge(xT_ready, 1 + KT)
                    if g0 == 0:
                        make_q(s + 1, s0 + 1)
                    pe.wait_ge(qk_ready, s + 1)
                    for j in range(NQ):
                        if g0 % 2 == 0 and r == 0:
                            pe.wait_ge(ctxT_ready, i * 8 + (g0 // 2 * NQ + j + 1))
                        wait(pe, exp_done, s * NQ + (j + 1 - NQ))
                        if has_att(g0) and j == 3 and r == 1:
                            pe.wait_ge(att_ready, i * 4 + (g0 - 1))
                        if has_out(g0) and j == 3 and r == 2:
                            pe.wait_ge(out_ready, i + (g0 - 1) // 4)
                        parts = [(qk_hi, ctxT_hi), (qk_lo, ctxT_hi), (qk_hi, ctxT_lo)]
                        for t in range(KT):
                            for n, (a, b) in enumerate(parts):
                                last = pe.matmul(ps_s[:, j, 0:QE[j]], a[:, t, :], b[:, t, keys(j)],
                                                 start=t == 0 and n == 0, stop=t == KT - 1 and n == 2)
                        last.then_inc(scores_ready, 1)
                        if g0 == 0 and j == 2:
                            make_qk(s + 1, s0 + 1)
                        if g0 == 0 and r == NR - 1 and j in (0, NQ - 1):
                            transpose_x(min(j, 1))
                        if has_pc(g0) and r == 0 and j in (1, 2):
                            transpose_chunk(j - 1)
                elif has_pc(g0) and r == 0:
                    transpose_chunk(0)
                    transpose_chunk(1)
                for n, c in enumerate(CHUNKS[r]):
                    if has_pc(g0):
                        if c + 2 < NC:
                            transpose_chunk(c + 2)
                        multiply_chunk(c)
                    if n == 0 and has_next_q(g0, r) and g0 > 0 and (s0 + 1) // 8 % 2 == 0:
                        if has_scores(g0):
                            pe.wait_ge(exp_done, s * NQ + 1)
                        make_q(s + 1, s0 + 1)
                    if n == 1 and has_next_q(g0, r) and g0 > 0:
                        if has_scores(g0):
                            pe.wait_ge(exp_done, s * NQ + 2)
                        make_qk(s + 1, s0 + 1)
                    if n == 2 and has_att(g0) and r == 0:
                        if g0 == 2:
                            pe.wait_ge(wvo_in, 32)
                        pe.wait_ge(pcT_ready, i * 4 + (g0 - 1))
                        if has_scores(g0):
                            pe.wait_ge(exp_done, s * NQ + NQ)
                        for m in range(4):
                            pair = 4 * (g0 % 2) + m
                            for e in range(2):
                                for t in range(KT):
                                    col = DH * (2 * pair + e)
                                    row = T * (2 * m + e)
                                    last = pe.matmul(ps_att[DH * e:DH * e + DH, T * m:T * m + T],
                                                     wv[:, t, col:col + DH], pcT[:, t, row:row + T],
                                                     start=t == 0, stop=t == KT - 1)
                        last.then_inc(att_ps, 1)
                    if n == 2 and has_out(g0) and r == 1:
                        pe.wait_ge(att_ready, i * 4 + (g0 - 1))
                        if has_scores(g0):
                            pe.wait_ge(exp_done, s * NQ + NQ)
                        for m in range(H // 2):
                            last = pe.matmul(ps_out, attT[:, m].rearrange("p b q -> p (b q)"), wo[:, m, :],
                                             start=m == 0, stop=m == H // 2 - 1)
                        last.then_inc(out_ps, 1)

            over_slots(pe, slot)


def self_attention_and_experts(nc, x1, stats, mv, lnt, alibi_d, WqkT, bqk, WV, bV, WoT, bo, gateT, gate_bias,
                               experts, ident, rank_d, diag_d, out):
    with ExitStack() as stack:
        def sb(name, shape, dt=F32):
            return stack.enter_context(nc.sbuf_tensor(name, shape, dt))

        def sem(name):
            return stack.enter_context(nc.semaphore(name))

        x1b = sb("x1b", [P, NT, D])
        x2 = sb("x2", [P, NT, D])
        xn = sb("xn", [P, NT, D])
        xnT = sb("xnT", [P, KT, TOK])
        wqk = sb("wqk", [P, KT, 4 * P])
        wvs = sb("wvs", [P, KT, 2 * P])
        woT = sb("woT", [P, KT, D])
        bqk_s = sb("bqk_s", [P, 4])
        bv = sb("bv", [P, P])
        bout = sb("bout", [P, D])
        alibi = sb("alibi", [P, H2 * T])
        rank = sb("rank", [P, NE])
        diag = sb("diag", [P, 8])
        qkT = sb("qkT", [P, 4, TOK])
        kd = sb("kd", [P, 2, 2, 2, 8, T])
        vs = sb("vs", [P, NB, P])
        vd = sb("vd", [P, 2, 4, 5 * P])
        pr = sb("pr", [P, 3, H2, T])
        prT = sb("prT", [P, 2, 8, P])
        oT = sb("oT", [P, 2, KT, P])
        pmax = sb("pmax", [P, 3, 16])
        psum_r = sb("psum_r", [P, 3, 16])
        pinv = sb("pinv", [P, 3, 16])
        xnT_hi = sb("xnT_hi", [P, KT, TOK], F32R)
        xnT_lo = sb("xnT_lo", [P, KT, TOK], F32R)
        gw = sb("gw", [P, KT, NE])
        gb = sb("gb", [P, NE])
        gt = pr[:, 0, 0:8, :].rearrange("p s (n e) -> p s n e", n=NT)
        gr = sb("gr", [P, 6, NT])
        gates = sb("gates", [P, NT, NX])
        w_raw = sb("w_raw", [P, 2, 6, D])
        w_hi = sb("w_hi", [P, 2, 6, D], F32R)
        w_lo = sb("w_lo", [P, 2, 6, D], F32R)
        act_a = qkT[:, 0].rearrange("p (m a) -> p m a", m=2)
        hid = qkT[:, 1].rearrange("p (m a) -> p m a", m=2)
        hid_hi = sb("hid_hi", [P, 2, KT, 512], F32R)
        hid_lo = sb("hid_lo", [P, 2, KT, 512], F32R)

        ps_a = stack.enter_context(nc.psum_tensor("ps_a", [P, 4, 512], F32))
        ps_b = stack.enter_context(nc.psum_tensor("ps_b", [P, 2, 512], F32))
        ps_c = stack.enter_context(nc.psum_tensor("ps_c", [P, 2, 512], F32))

        wv_in = sem("wv_in")
        wrest_in = sem("wrest_in")
        ew_in = [sem(f"ew_in{e}") for e in range(2)]
        chain_s = sem("dve_chain2")
        x1b_ready = sem("x1b_ready")
        var_ready = sem("var_ready2")
        root_ready = sem("root_ready2")
        xn_ready = sem("xn_ready2")
        xnT_ps = sem("xnT_ps")
        xnT_ready = sem("xnT_ready")
        wqk_in = sem("wqk_in")
        bout_in = sem("bout_in")
        qk_ps = sem("qk_ps2")
        qkT_ready = sem("qkT_ready")
        zeros_set = sem("zeros_set")
        kd_pool = sem("kd_pool")
        kd_dve = sem("kd_dve")
        vd_ready = sem("vd_ready")
        v_ps = sem("v_ps")
        v_ready = sem("v_ready")
        sc_ps = sem("sc_ps")
        sc_ready = sem("sc_ready")
        pmax_ready = sem("pmax_ready")
        shifted = sem("shifted")
        p_exp = sem("p_exp")
        psum_ready = sem("psum_ready")
        pinv_ready = sem("pinv_ready")
        p_ready = sem("p_ready")
        prT_ps = sem("prT_ps")
        prT_ready = sem("prT_ready")
        o_ps = sem("o_ps")
        oT_ready = sem("oT_ready")
        y_ps = sem("y_ps")
        x2_ready = sem("x2_ready")
        x2_stats_ready = sem("x2_stats_ready")
        xnT_hi_ready = sem("xnT_hi_ready")
        xnT_lo_ready = sem("xnT_lo_ready")
        gl_ps = sem("gl_ps")
        gl_shifted = sem("gl_shifted")
        gl_exp = sem("gl_exp")
        ewh_ready = sem("ewh_ready")
        ew_ready = sem("ew_ready")
        ab2_ps = sem("ab2_ps")
        silu_ready = sem("silu_ready")
        hid_ready = sem("hid_ready")
        hid_hi_ready = sem("hid_hi_ready")
        hid_lo_ready = sem("hid_lo_ready")
        ey_ps = sem("ey_ps")
        acc_ready = sem("acc_ready")
        stored = sem("stored")
        ones_set = sem("ones_set")

        def wait(eng, s, count):
            if not isinstance(count, int) or count > 0:
                eng.wait_ge(s, count)

        block = stack.enter_context(nc.Block())

        def ps_qk(n):
            return ps_a[:, n, :] if n < 4 else ps_c[:, n % 2, :]

        def diagonal(eng, i, e):
            for o in range(2):
                k = qkT[:, 2 + o, T * (2 * i + e):T * (2 * i + e) + T]
                last = eng.tensor_tensor(kd[:, i % 2, e, o], k.unsqueeze(1).to_broadcast([P, 8, T]),
                                         diag[:].unsqueeze(2).to_broadcast([P, 8, T]), ALU.mult)
            return last

        @block.sync
        def _(sp):
            sp.dma_start(wqk[:], WqkT.rearrange("(t p) n -> p t n", p=P)).then_inc(wqk_in, 16)
            sp.dma_start(bqk_s[:], bqk).then_inc(wqk_in, 16)
            sp.dma_start(bout[:], bo.partition_broadcast(P)).then_inc(bout_in, 16)
            sp.dma_start(wvs[:], WV.rearrange("(t p) n -> p t n", p=P)).then_inc(wv_in, 16)
            sp.dma_start(diag[:], diag_d).then_inc(wv_in, 16)
            for e in range(2):
                sp.dma_start(bv[T * e:T * e + T, :], bV[e].partition_broadcast(T)).then_inc(wv_in, 16)
            for e in range(2):
                sp.dma_start(alibi[T * e:T * e + T, :], alibi_d).then_inc(wv_in, 16)
            sp.dma_start(woT[:], WoT.rearrange("(t p) n -> p t n", p=P)).then_inc(wrest_in, 16)
            sp.dma_start(gw[:], gateT.rearrange("(t p) n -> p t n", p=P)).then_inc(wrest_in, 16)
            sp.dma_start(gb[:], gate_bias.partition_broadcast(P)).then_inc(wrest_in, 16)
            sp.dma_start(rank[:], rank_d.partition_broadcast(P)).then_inc(wrest_in, 16)
            ew = experts.rearrange("x (w p) d -> x p w d", p=P)
            for e in range(2):
                sp.dma_start(w_raw[:, e], ew[e]).then_inc(ew_in[e], 16)
            with sp.Fori(0, NX // 2 - 1) as i:
                for e in range(2):
                    sp.wait_ge(ew_ready, i * 2 + (e + 1))
                    sp.dma_start(w_raw[:, e], ew[bass.ds(i * 2 + (2 + e), 1)].rearrange("x p w d -> p (x w) d")
                                 ).then_inc(ew_in[e], 16)
            outr = out.rearrange("(n p) d -> p n d", p=P)
            for h in range(2):
                for n in range(4):
                    sp.wait_ge(acc_ready, 8 * (NX - 1) + 4 * h + n + 1)
                    sp.dma_start(outr[:, 4 * h + n, :], x2[:, 4 * h + n, :]).then_inc(stored, 16)
            sp.wait_ge(stored, 16 * NT)

        @block.gpsimd
        def _(pool):
            pool.memset(gates[:, :, NE:NX], 1.0).then_inc(ones_set, 1)
            pool.memset(vd[:], 0.0).then_inc(zeros_set, 1)
            pool.wait_ge(bout_in, 16)
            for n in range(NT):
                pool.tensor_tensor(x1b[:, n, :], x1[:, n, :], bout[:], ALU.add).then_inc(x1b_ready, 1)

            def diagonals(i):
                if i == 0:
                    pool.wait_ge(wv_in, 96)
                if i % 4 == 0:
                    pool.wait_ge(qkT_ready, i + 4)
                if i >= 2:
                    pool.wait_ge(sc_ps, i - 1)
                diagonal(pool, i, 0).then_inc(kd_pool, 1)

            def normalise(i):
                pool.wait_ge(pinv_ready, i + 1)
                pool.tensor_tensor(pr[:, i % 3], pr[:, i % 3], pinv[:, i % 3, :].unsqueeze(2).to_broadcast([P, 16, T]),
                                   ALU.mult).then_inc(p_ready, 1)

            def expert_weights(i, e):
                pool.wait_ge(ewh_ready, i * 2 + (e + 1))
                pool.tensor_tensor(w_lo[:, e % 2], w_raw[:, e % 2], w_hi[:, e % 2].bitcast(F32), ALU.subtract
                                   ).then_inc(ew_ready, 1)

            def split_xnT(m):
                t, cols = m % 2, slice(512 * (m // 2), 512 * (m // 2) + 512)
                pool.wait_ge(xnT_hi_ready, m + 1)
                pool.tensor_tensor(xnT_lo[:, t, cols], xnT[:, t, cols], xnT_hi[:, t, cols].bitcast(F32),
                                   ALU.subtract).then_inc(xnT_lo_ready, 1)

            diagonals(0)
            diagonals(1)
            for i in range(NT):
                pool.wait_ge(pmax_ready, i + 1)
                pool.tensor_tensor(pr[:, i % 3], pr[:, i % 3], pmax[:, i % 3, :].unsqueeze(2).to_broadcast([P, 16, T]),
                                   ALU.subtract).then_inc(shifted, 1)
                if i >= 1:
                    normalise(i - 1)
                if i + 2 < NT:
                    diagonals(i + 2)
                if i == NT - 2:
                    expert_weights(0, 0)
            normalise(NT - 1)
            for m in range(4):
                split_xnT(m)
            expert_weights(0, 1)
            with pool.Fori(1, NX // 2) as i:
                for e in range(2):
                    expert_weights(i, e)

        @block.scalar
        def _(act):
            def roots(n, cols):
                act.wait_ge(var_ready, n + 1)
                act.activation(lnt[:, 1, cols], lnt[:, 0, cols], ACT.Sqrt).then_inc(root_ready, 1)

            roots(0, slice(NT - 1, NT))
            act.wait_ge(wqk_in, 32)

            def take_qk(n):
                act.wait_ge(qk_ps, n + 1)
                act.activation(qkT[:, n % 4, 512 * (n // 4):512 * (n // 4) + 512], ps_qk(n), ACT.Identity,
                               bias=bqk_s[:, n % 4:n % 4 + 1]).then_inc(qkT_ready, 1)

            for n in range(4):
                take_qk(n)

            def split_xnT(m):
                t, cols = m % 2, slice(512 * (m // 2), 512 * (m // 2) + 512)
                act.wait_ge(xnT_ready, 4 + m + 1)
                act.activation(xnT_hi[:, t, cols], xnT[:, t, cols], ACT.Copy).then_inc(xnT_hi_ready, 1)

            def split_weights(i, e):
                act.wait_ge(ew_in[e % 2], i * 16 + 16 * (e // 2 + 1))
                wait(act, ey_ps, i * 16 + 8 * (e - 1))
                act.activation(w_hi[:, e % 2], w_raw[:, e % 2], ACT.Copy).then_inc(ewh_ready, 1)

            def exp(i):
                act.wait_ge(shifted, i + 1)
                act.activation(pr[:, i % 3], pr[:, i % 3], ACT.Exp).then_inc(p_exp, 1)

            def take_oT(i):
                act.wait_ge(o_ps, i + 1)
                act.activation(oT[:, i % 2].rearrange("p t q -> p (t q)"), ps_c[:, i % 2, 0:KT * P], ACT.Copy
                               ).then_inc(oT_ready, 1)

            def take_prT(i):
                for w in range(2):
                    act.wait_ge(prT_ps, 2 * i + w + 1)
                    act.activation(prT[:, i % 2, 4 * w:4 * w + 4, :].rearrange("p m q -> p (m q)"), ps_b[:, w, :],
                                   ACT.Copy).then_inc(prT_ready, 1)

            def values(i):
                act.wait_ge(v_ready, i // 2 + 1)
                if i == 0:
                    act.wait_ge(zeros_set, 1)
                if i >= 2:
                    act.wait_ge(o_ps, i - 1)
                for o in range(2):
                    half = slice(T * o, T * o + T)
                    to = vd[half, i % 2].rearrange("p x (m c) -> p x m c", m=4)[:, :, :, DH2 * o:DH2 * o + DH2]
                    v = vs[half, 2 * i:2 * i + 2, :].rearrange("p e (w m c) -> p (e w) m c", w=2, m=4)
                    act.activation(to, v, ACT.Copy).then_inc(vd_ready, 1)

            split_weights(0, 0)
            take_qk(4)
            take_qk(5)
            for i in range(NT + 2):
                if i < NT:
                    exp(i)
                if i == 0:
                    take_qk(6)
                    take_qk(7)
                if i >= 2:
                    take_oT(i - 2)
                if 1 <= i <= NT:
                    take_prT(i - 1)
                if i < NT:
                    values(i)
                if i == NT - 2:
                    roots(1, slice(0, NT // 2))
                if i == NT:
                    split_xnT(0)
                    split_xnT(1)
            roots(2, slice(NT // 2, NT))

            def silu(i, e, h, m):
                act.wait_ge(ab2_ps, i * 8 + (4 * e + 2 * h + m + 1))
                act.activation(act_a[:, m, :], ps_a[:, 2 * m, :], ACT.Silu).then_inc(silu_ready, 1)

            def split_hidden(i, e, h, m):
                act.wait_ge(hid_ready, i * 8 + (4 * e + 2 * h + m + 1))
                act.activation(hid_hi[:, h, m, :], hid[:, m, :], ACT.Copy).then_inc(hid_hi_ready, 1)

            def hidden(i, e, h):
                wait(act, ey_ps, i * 16 + (8 * (e - 1) + 4 * h + 4))
                for m in range(KT):
                    silu(i, e, h, m)
                    split_hidden(i, e, h, m)

            def two_experts(i, last):
                for e in range(2):
                    if isinstance(i, int) and i == 0 and e == 0:
                        silu(0, 0, 0, 0)
                        split_hidden(0, 0, 0, 0)
                        silu(0, 0, 0, 1)
                        split_xnT(2)
                        split_xnT(3)
                        split_hidden(0, 0, 0, 1)
                        act.wait_ge(gl_shifted, 1)
                        act.activation(gt[:, 1], gt[:, 0], ACT.Exp).then_inc(gl_exp, 1)
                    else:
                        hidden(i, e, 0)
                    if not (last and e == 1):
                        split_weights(i, e + 1)
                    hidden(i, e, 1)

            two_experts(0, False)
            with act.Fori(1, NX // 2 - 1) as i:
                two_experts(i, False)
            two_experts(NX // 2 - 1, True)

        @block.vector
        def _(dve):
            chain = [0]

            def link(ins):
                chain[0] += 1
                ins.then_inc(chain_s, 1)
                dve.wait_ge(chain_s, chain[0])

            def inverse_roots(k, tiles):
                cols = slice(tiles[0], tiles[-1] + 1)
                for n in tiles:
                    last = dve.bn_aggr(mv[:, n, :], stats[:, n, :])
                link(last)
                dve.tensor_scalar(lnt[:, 0, cols], mv[:, cols, 1], EPS, None, ALU.add).then_inc(var_ready, 1)
                dve.wait_ge(var_ready, k + 1)
                dve.wait_ge(root_ready, k + 1)
                link(dve.reciprocal(lnt[:, 2, cols], lnt[:, 1, cols]))
                link(dve.tensor_tensor(lnt[:, 3, cols], lnt[:, 0, cols], lnt[:, 2, cols], ALU.mult))
                link(dve.tensor_tensor(lnt[:, 4, cols], lnt[:, 3, cols], lnt[:, 1, cols], ALU.add))
                link(dve.tensor_scalar(lnt[:, 5, cols], lnt[:, 4, cols], 0.5, None, ALU.mult))
                link(dve.reciprocal(lnt[:, 2, cols], lnt[:, 5, cols]))

            def normalise(rows, tiles):
                for n in tiles:
                    dve.tensor_scalar(xn[:, n, :], rows[:, n, :], mv[:, n, 0:1], lnt[:, 2, n:n + 1],
                                      ALU.subtract, ALU.mult).then_inc(xn_ready, 1)

            def take_xnT(k, h, ps):
                for t in range(KT):
                    dve.wait_ge(xnT_ps, 4 * k + 2 * h + t + 1)
                    dve.tensor_copy(xnT[:, t, 512 * h:512 * h + 512], ps[:, t, :]).then_inc(xnT_ready, 1)

            normalise(x1, range(NT // 2))
            take_xnT(0, 0, ps_a[:, 0:2])
            inverse_roots(0, range(NT - 1, NT))
            normalise(x1, range(NT // 2, NT))
            take_xnT(0, 1, ps_c)

            def diagonals(i):
                if i == 0:
                    dve.wait_ge(wv_in, 96)
                if i % 4 == 0:
                    dve.wait_ge(qkT_ready, i + 4)
                if i >= 2:
                    dve.wait_ge(sc_ps, i - 1)
                diagonal(dve, i, 1).then_inc(kd_dve, 1)

            def take_v(n):
                dve.wait_ge(v_ps, n + 1)
                dve.tensor_tensor(vs[:, 4 * n:4 * n + 4, :], ps_b[:, n % 2, :].rearrange("p (b c) -> p b c", b=4),
                                  bv[:].unsqueeze(1).to_broadcast([P, 4, P]), ALU.add).then_inc(v_ready, 1)

            def scores(i):
                s = pr[:, i % 3]
                dve.wait_ge(sc_ps, i + 1)
                if i >= 3:
                    dve.wait_ge(prT_ps, 2 * (i - 2))
                dve.scalar_tensor_tensor(s.rearrange("p h k -> p (h k)"),
                                         ps_a[:, 2 * (i % 2):2 * (i % 2) + 2, :].rearrange("p w c -> p (w c)"),
                                         SCALE2, alibi[:], ALU.mult, ALU.add).then_inc(sc_ready, 1)
                dve.wait_ge(sc_ready, i + 1)
                dve.tensor_reduce(pmax[:, i % 3, :], s, AX.X, ALU.max).then_inc(pmax_ready, 1)

            def sums(i):
                dve.wait_ge(p_exp, i + 1)
                dve.tensor_reduce(psum_r[:, i % 3, :], pr[:, i % 3], AX.X, ALU.add).then_inc(psum_ready, 1)
                dve.wait_ge(psum_ready, i + 1)
                dve.reciprocal(pinv[:, i % 3, :], psum_r[:, i % 3, :]).then_inc(pinv_ready, 1)

            def residual(i):
                dve.wait_ge(x1b_ready, i + 1)
                dve.wait_ge(y_ps, i + 1)
                dve.tensor_tensor(x2[:, i, :], ps_c[:, i % 2, D:2 * D], x1b[:, i, :], ALU.add).then_inc(x2_ready, 1)
                dve.wait_ge(x2_ready, i + 1)
                dve.bn_stats(stats[:, i, :], x2[:, i, :]).then_inc(x2_stats_ready, 1)

            diagonals(0)
            take_v(0)
            take_v(1)
            diagonals(1)
            scores(0)
            diagonals(2)
            scores(1)
            for i in range(NT + 1):
                if i < NT:
                    sums(i)
                if i == 0:
                    for n in range(2, NB // 4):
                        take_v(n)
                if i + 3 < NT:
                    diagonals(i + 3)
                if i + 2 < NT:
                    scores(i + 2)
                if i == NT - 2:
                    dve.wait_ge(x2_stats_ready, NT // 2)
                    inverse_roots(1, range(NT // 2))
                    normalise(x2, range(NT // 2))
                if i >= 1:
                    residual(i - 1)
                if i == NT - 1:
                    take_xnT(1, 0, ps_a[:, 0:2])
            dve.wait_ge(x2_stats_ready, NT)
            inverse_roots(2, range(NT // 2, NT))
            normalise(x2, range(NT // 2, NT))

            def hidden_unit(i, e, h, m):
                unit = i * 8 + (4 * e + 2 * h + m)
                dve.wait_ge(silu_ready, unit + 1)
                dve.tensor_tensor(hid[:, m, :], act_a[:, m, :], ps_a[:, 2 * m + 1, :], ALU.mult
                                  ).then_inc(hid_ready, 1)
                dve.wait_ge(hid_hi_ready, unit + 1)
                dve.tensor_tensor(hid_lo[:, h, m, :], hid[:, m, :], hid_hi[:, h, m, :].bitcast(F32),
                                  ALU.subtract).then_inc(hid_lo_ready, 1)

            hidden_unit(0, 0, 0, 0)
            take_xnT(1, 1, ps_b)
            hidden_unit(0, 0, 0, 1)

            def over_e(a):
                return a.unsqueeze(2).to_broadcast([P, NT, NE])

            def over_n(a):
                return a.unsqueeze(1).to_broadcast([P, NT, NE])

            dve.wait_ge(gl_ps, 1)
            logits = ps_c[:, 0, 0:NT * NE].rearrange("p (n e) -> p n e", n=NT)
            link(dve.tensor_reduce(gr[:, 0, :], logits, AX.X, ALU.max))
            dve.tensor_tensor(gt[:, 0], logits, over_e(gr[:, 0, :]), ALU.subtract).then_inc(gl_shifted, 1)
            dve.wait_ge(gl_exp, 1)
            link(dve.tensor_reduce(gr[:, 1, :], gt[:, 1], AX.X, ALU.add))
            link(dve.reciprocal(gr[:, 2, :], gr[:, 1, :]))
            link(dve.tensor_tensor(gt[:, 2], gt[:, 1], over_e(gr[:, 2, :]), ALU.mult))
            dve.wait_ge(wrest_in, 64)
            link(dve.tensor_tensor(gt[:, 3], gt[:, 2], over_n(gb[:]), ALU.add))
            for k in range(2):
                biased, chosen = gt[:, 3], gt[:, 6 + k]
                link(dve.tensor_reduce(gr[:, 3, :], biased, AX.X, ALU.max))
                link(dve.tensor_tensor(gt[:, 4], biased, over_e(gr[:, 3, :]), ALU.is_ge))
                link(dve.tensor_tensor(gt[:, 5], gt[:, 4], over_n(rank[:]), ALU.mult))
                link(dve.tensor_reduce(gr[:, 4, :], gt[:, 5], AX.X, ALU.max))
                link(dve.tensor_tensor(chosen, gt[:, 5], over_e(gr[:, 4, :]), ALU.is_ge))
                if k == 0:
                    link(dve.scalar_tensor_tensor(biased, chosen, -BIG, biased, ALU.mult, ALU.add))
            link(dve.tensor_tensor(gt[:, 4], gt[:, 6], gt[:, 7], ALU.add))
            link(dve.tensor_tensor(gates[:, :, 0:NE], gt[:, 4], gt[:, 2], ALU.mult))

            def hidden(i, e, h):
                for m in range(KT):
                    hidden_unit(i, e, h, m)

            def accumulate(i, e, h):
                for n in range(4):
                    tile = 4 * h + n
                    dve.wait_ge(ey_ps, i * 16 + (8 * e + tile + 1))
                    wait(dve, acc_ready, i * 16 + (8 * e + tile + 1 - NT))
                    y = (ps_b, ps_c)[n // 2][:, n % 2, 0:D]
                    g = gates[:, tile, bass.ds(i * 2 + e, 1)]
                    dve.scalar_tensor_tensor(x2[:, tile, :], y, g, x2[:, tile, :], ALU.mult, ALU.add
                                             ).then_inc(acc_ready, 1)

            dve.wait_ge(ones_set, 1)
            hidden(0, 0, 1)
            accumulate(0, 0, 0)
            hidden(0, 1, 0)
            accumulate(0, 0, 1)
            hidden(0, 1, 1)
            accumulate(0, 1, 0)
            with dve.Fori(1, NX // 2) as i:
                hidden(i, 0, 0)
                accumulate(i - 1, 1, 1)
                hidden(i, 0, 1)
                accumulate(i, 0, 0)
                hidden(i, 1, 0)
                accumulate(i, 0, 1)
                hidden(i, 1, 1)
                accumulate(i, 1, 0)
            accumulate(NX // 2 - 1, 1, 1)

        @block.tensor
        def _(pe):
            def transpose_xn(k, h, ps):
                for t in range(KT):
                    for n in range(4):
                        pe.wait_ge(xn_ready, NT * k + 4 * h + n + 1)
                        last = pe.transpose(ps[:, t, P * n:P * n + P], xn[:, 4 * h + n, P * t:P * t + P], ident[:])
                    last.then_inc(xnT_ps, 1)

            transpose_xn(0, 0, ps_a[:, 0:2])
            def make_qk(n):
                for t in range(KT):
                    last = pe.matmul(ps_qk(n), wqk[:, t, P * (n % 4):P * (n % 4) + P],
                                     xnT[:, t, 512 * (n // 4):512 * (n // 4) + 512], start=t == 0, stop=t == KT - 1)
                last.then_inc(qk_ps, 1)

            pe.wait_ge(wqk_in, 32)
            pe.wait_ge(xnT_ready, 2)
            for n in range(4):
                make_qk(n)
            transpose_xn(0, 1, ps_c)

            def make_v(n):
                if n >= 2:
                    pe.wait_ge(v_ready, n - 1)
                for b in range(4 * n, 4 * n + 4):
                    for o in range(2):
                        for t in range(KT):
                            last = pe.matmul(ps_b[T * o:T * o + T, n % 2, P * (b % 4):P * (b % 4) + P],
                                             xnT[:, t, T * b:T * b + T], wvs[:, t, P * o:P * o + P],
                                             start=t == 0, stop=t == KT - 1)
                last.then_inc(v_ps, 1)

            def scores(i):
                pe.wait_ge(kd_pool, i + 1)
                pe.wait_ge(kd_dve, i + 1)
                if i < 2:
                    pe.wait_ge(qkT_ready, 4)
                else:
                    pe.wait_ge(sc_ready, i - 1)
                for e in range(2):
                    tok = slice(T * (2 * i + e), T * (2 * i + e) + T)
                    for o in range(2):
                        last = pe.matmul(ps_a[T * e:T * e + T, 2 * (i % 2) + o, :], qkT[:, o, tok],
                                         kd[:, i % 2, e, o].rearrange("p h k -> p (h k)"), start=True, stop=True)
                last.then_inc(sc_ps, 1)

            def transpose_probs(i):
                pe.wait_ge(p_ready, i + 1)
                if i >= 1:
                    pe.wait_ge(prT_ready, 2 * i)
                else:
                    pe.wait_ge(v_ready, 4)
                for w in range(2):
                    for m in range(4):
                        h = 8 * w + 2 * m
                        last = pe.transpose(ps_b[:, w, P * m:P * m + P],
                                            pr[:, i % 3, h:h + 2, :].rearrange("p h k -> p (h k)"), ident[:])
                    last.then_inc(prT_ps, 1)

            def multiply_v(i):
                pe.wait_ge(vd_ready, 2 * i + 2)
                if i >= 2:
                    pe.wait_ge(x2_ready, i - 1)
                elif i == 0:
                    pe.wait_ge(qkT_ready, 8)
                for w in range(2):
                    pe.wait_ge(prT_ready, 2 * i + w + 1)
                    for e in range(2):
                        for m in range(4):
                            last = pe.matmul(ps_c[:, i % 2, P * w + T * e:P * w + T * e + T],
                                             vd[:, i % 2, 2 * e + w, P * m:P * m + P],
                                             prT[:, i % 2, 4 * w + m, T * e:T * e + T], start=m == 0, stop=m == 3)
                last.then_inc(o_ps, 1)

            def project(i):
                pe.wait_ge(oT_ready, i + 1)
                for t in range(KT):
                    last = pe.matmul(ps_c[:, i % 2, D:2 * D], oT[:, i % 2, t, :], woT[:, t, :], start=t == 0,
                                     stop=t == KT - 1)
                last.then_inc(y_ps, 1)

            pe.wait_ge(wv_in, 96)
            make_v(0)
            make_v(1)
            scores(0)
            scores(1)
            pe.wait_ge(xnT_ready, 4)
            for n in range(4, 8):
                if n >= 6:
                    pe.wait_ge(qkT_ready, n - 1)
                make_qk(n)
            make_v(2)
            make_v(3)
            pe.wait_ge(wrest_in, 64)
            for i in range(NT + 1):
                if i + 2 < NT:
                    scores(i + 2)
                if i == NT - 1:
                    pe.wait_ge(sc_ready, NT)
                    transpose_xn(1, 0, ps_a[:, 0:2])
                if i < NT:
                    transpose_probs(i)
                if i >= 1:
                    project(i - 1)
                if i < NT:
                    multiply_v(i)

            def router(tiles):
                for n in tiles:
                    for t in range(KT):
                        last = pe.matmul(ps_c[:, 0, NE * n:NE * n + NE], xnT[:, t, P * n:P * n + P], gw[:, t, :],
                                         start=t == 0, stop=t == KT - 1)
                return last

            def hidden(i, e, h):
                if h == 0:
                    pe.wait_ge(ew_ready, i * 2 + (e + 1))
                for m in range(KT):
                    unit = i * 8 + (4 * e + 2 * h + m)
                    wait(pe, hid_ready, unit - 1)
                    for k in range(2):
                        for t in range(KT):
                            parts = [(w_hi, xnT_hi), (w_lo, xnT_hi), (w_hi, xnT_lo)]
                            for n, (a, b) in enumerate(parts):
                                last = pe.matmul(ps_a[:, 2 * m + k, :], a[:, e, 2 * k + t, P * m:P * m + P],
                                                 b[:, t, 512 * h:512 * h + 512],
                                                 start=t == 0 and n == 0, stop=t == KT - 1 and n == 2)
                    last.then_inc(ab2_ps, 1)

            def outputs(i, e, h):
                unit = i * 8 + (4 * e + 2 * h)
                pe.wait_ge(hid_lo_ready, unit + 2)
                for n in range(4):
                    tile = 4 * h + n
                    wait(pe, acc_ready, i * 16 + (8 * e + tile + 1 - 4))
                    for t in range(KT):
                        parts = [(hid_hi, w_hi), (hid_lo, w_hi), (hid_hi, w_lo)]
                        for k, (a, b) in enumerate(parts):
                            last = pe.matmul((ps_b, ps_c)[n // 2][:, n % 2, 0:D], a[:, h, t, P * n:P * n + P],
                                             b[:, e, 4 + t, :], start=t == 0 and k == 0,
                                             stop=t == KT - 1 and k == 2)
                    last.then_inc(ey_ps, 1)

            pe.wait_ge(xnT_lo_ready, 2)
            hidden(0, 0, 0)
            transpose_xn(1, 1, ps_b)
            pe.wait_ge(x2_ready, NT - 1)
            router(range(NT // 2))
            pe.wait_ge(xnT_ready, 8)
            router(range(NT // 2, NT)).then_inc(gl_ps, 1)
            pe.wait_ge(xnT_lo_ready, 4)
            hidden(0, 0, 1)
            pe.wait_ge(gl_shifted, 1)
            outputs(0, 0, 0)
            hidden(0, 1, 0)
            outputs(0, 0, 1)
            hidden(0, 1, 1)
            outputs(0, 1, 0)
            with pe.Fori(1, NX // 2) as i:
                hidden(i, 0, 0)
                outputs(i - 1, 1, 1)
                hidden(i, 0, 1)
                outputs(i, 0, 0)
                hidden(i, 1, 0)
                outputs(i, 0, 1)
                hidden(i, 1, 1)
                outputs(i, 1, 0)
            outputs(NX // 2 - 1, 1, 1)


def program(nc, x, ctxT, ctx, Wq, WkT, Wv, Wo, alibi, WqkT, bqk, WV, bV, WoT, bo, gateT, gate_bias,
            experts, ident, rank, diag, out):
    with ExitStack() as stack:
        x1 = stack.enter_context(nc.sbuf_tensor("x1", [P, NT, D], F32))
        ident_s = stack.enter_context(nc.sbuf_tensor("ident", [P, P], F32))
        stats = stack.enter_context(nc.sbuf_tensor("stats", [P, NT, 6], F32))
        mv = stack.enter_context(nc.sbuf_tensor("mv", [P, NT, 2], F32))
        lnt = stack.enter_context(nc.sbuf_tensor("lnt", [P, 6, NT], F32))
        cross_attention(nc, x, ctxT, ctx, Wq, WkT, Wv, Wo, ident, ident_s, x1, stats, mv, lnt)
        self_attention_and_experts(nc, x1, stats, mv, lnt, alibi, WqkT, bqk, WV, bV, WoT, bo, gateT, gate_bias,
                                   experts, ident_s, rank, diag, out)


def layouts(v):
    qkv = v["L0_attn_qkv_w"].reshape(H2, 3 * DH2, D)
    qkv_b = v["L0_attn_qkv_b"].reshape(H2, 3 * DH2)

    def even_odd(a):
        return a.reshape(2, 4, 2, *a.shape[1:]).transpose(2, 0, 1, *range(3, a.ndim + 2))

    pos = np.arange(T, dtype=np.float32)
    slopes = np.float32(0.5) ** np.arange(H2, dtype=np.float32)
    dist = -np.abs(pos[:, None] - pos[None, :])[:, None, :] * slopes[None, :, None]
    return {
        "x": v["x"].reshape(TOK, D),
        "ctxT": v["ctx_1024"].transpose(0, 2, 1),
        "ctx": v["ctx_1024"],
        "Wq": v["L0_xattn_Wq"],
        "WkT": v["L0_xattn_Wk"].T,
        "Wv": v["L0_xattn_Wv"],
        "Wo": v["L0_xattn_Wo"],
        "alibi": dist.reshape(T, H2 * T),
        "WqkT": qkv[:, 0:2 * DH2].reshape(H2, 2, DH2, D).transpose(1, 0, 2, 3).reshape(4 * P, D).T,
        "bqk": qkv_b[:, 0:2 * DH2].reshape(H2, 2, DH2).transpose(1, 0, 2).reshape(4, P).T,
        "WV": even_odd(qkv[:, 2 * DH2:]).reshape(D, D).T,
        "bV": even_odd(qkv_b[:, 2 * DH2:]).reshape(2, P),
        "WoT": v["L0_attn_out_w"].T,
        "bo": v["L0_attn_out_b"],
        "gateT": v["L0_ffn_gate_w"].T,
        "gate_bias": v["L0_ffn_gate_bias"],
        "experts": np.concatenate([
            np.concatenate([v["L0_ffn_w1"].transpose(0, 2, 1), v["L0_ffn_w3"].transpose(0, 2, 1),
                            v["L0_ffn_w2"].transpose(0, 2, 1)], axis=1),
            np.concatenate([v["L0_ffn_sw1"].reshape(NSH, INTER, D).transpose(0, 2, 1),
                            v["L0_ffn_sw3"].reshape(NSH, INTER, D).transpose(0, 2, 1),
                            v["L0_ffn_sw2"].T.reshape(NSH, INTER, D)], axis=1)], axis=0),
        "ident": np.eye(P, dtype=np.float32),
        "rank": np.arange(NE, 0, -1, dtype=np.float32),
        "diag": np.repeat(np.eye(8, dtype=np.float32), DH2, axis=0),
    }


def kernel(**inputs):
    import numpy as _np
    import concourse.bacc as _bacc
    from concourse import mybir as _mybir
    from concourse.bass_utils import run_bass_kernel_spmd as _run

    nc = _bacc.Bacc("TRN2", target_bir_lowering=False, num_devices=1)
    arrays, args = {}, {}
    for name, a in layouts({k: _np.asarray(v) for k, v in inputs.items()}).items():
        a = _np.ascontiguousarray(a)
        arrays[f"in_{name}_dram"] = a
        args[name] = nc.dram_tensor(f"in_{name}_dram", a.shape, _mybir.dt.from_np(a.dtype), kind="ExternalInput").ap()
    out = nc.dram_tensor("out_0_dram", (TOK, D), _mybir.dt.float32, kind="ExternalOutput").ap()
    program(nc, out=out, **args)
    r = _run(nc, [arrays], core_ids=[0])
    return r.results[0]["out_0_dram"].reshape(NB, T, D)
```
